# Optimizing a Trainium2 kernel written in Bass

```python
import numpy as np
import jax
import jax.numpy as jnp

def _softmax(x, axis=-1):
    return jax.nn.softmax(x, axis=axis)

def _gelu(x):
    return jax.nn.gelu(x, approximate=True)

def _silu(x):
    return jax.nn.silu(x)

def _sigmoid(x):
    return jax.nn.sigmoid(x)

def _layernorm(x, axis=-1, eps=1e-05):
    m = jnp.mean(x, axis=axis, keepdims=True)
    v = jnp.var(x, axis=axis, keepdims=True)
    return (x - m) / jnp.sqrt(v + eps)

def _scatter_add(tgt, idx, src, axis=0):
    return tgt.at[idx].add(src)

def _segment_sum(src, seg, n):
    return jax.ops.segment_sum(src, seg, n)
kernel_name = 'mk_adj_seq_d2_adj_r2_4c0839'

def setup_inputs(seed: int=0):
    np.random.seed(seed)
    _w = jnp.asarray

    def _rec_inputs():
        import jax
        import jax.numpy as jnp
        _gk = jax.random.key(seed)
        x = -0.0005207 + 1.001 * jax.random.normal(jax.random.fold_in(_gk, 1), (8, 2048, 128), jnp.float32)
        _a = jax.random.bernoulli(jax.random.fold_in(_gk, 2), 0.000976562, (8, 2048, 2048))
        _a = jnp.logical_or(_a, jnp.swapaxes(_a, -1, -2))
        _a = jnp.logical_or(_a, jnp.eye(2048, dtype=bool))
        _af = _a.astype(jnp.float32)
        _af = _af * jax.random.uniform(jax.random.fold_in(_gk, 3), (8, 2048, 2048), jnp.float32, 0.05, 1)
        adj = _af
        return (x, adj)
    x, adj = _rec_inputs()

    def _L0_gnn_setup():
        import jax, jax.numpy as jnp
        import numpy as np
        ALPHA = 0.2
        key = jax.random.key(seed)
        ks = jax.random.split(key, 6)
        B, N, F_IN, F_OUT = (4, 2048, 128, 128)
        return {'input': jax.random.normal(ks[0], (B, N, F_IN), dtype=jnp.float32), 'adj': jax.random.uniform(ks[1], (B, N, N), dtype=jnp.float32), 'W': jax.random.normal(ks[2], (F_IN, F_OUT), dtype=jnp.float32) * (np.sqrt(2.0) / np.sqrt(F_IN)), 'a1': jax.random.normal(ks[3], (F_OUT, 1), dtype=jnp.float32) * 0.1, 'a2': jax.random.normal(ks[4], (F_OUT, 1), dtype=jnp.float32) * 0.1, 'bias': jax.random.normal(ks[5], (N, F_OUT), dtype=jnp.float32) * 0.02}
    _L0_gnn_all = _L0_gnn_setup()
    _L0_gnn_in = {k: v for k, v in _L0_gnn_all.items() if k in ('W', 'a1', 'a2', 'bias')}
    del _L0_gnn_all

    def _L1_gnn_setup():
        import jax, jax.numpy as jnp
        import numpy as np
        BN_EPS = 1e-05
        key = jax.random.key(seed)
        k1, k2, k3, k4 = jax.random.split(key, 4)
        B, N, F = (4, 2048, 128)
        x = jax.random.normal(k1, (B, N, F), dtype=jnp.float32)
        adj = jax.random.uniform(k2, (B, N, N), dtype=jnp.float32)
        W = jax.random.normal(k3, (F, F), dtype=jnp.float32) * (1.0 / np.sqrt(F))
        b = jax.random.normal(k4, (F,), dtype=jnp.float32) * 0.01
        gamma = jnp.ones((F,), dtype=jnp.float32)
        beta = jnp.zeros((F,), dtype=jnp.float32)
        return {'x': x, 'adj': adj, 'W': W, 'b': b, 'gamma': gamma, 'beta': beta}
    _L1_gnn_all = _L1_gnn_setup()
    _L1_gnn_in = {k: v for k, v in _L1_gnn_all.items() if k in ('W', 'b', 'gamma', 'beta')}
    del _L1_gnn_all
    return {'x': x, 'adj': adj, 'L0_gnn_W': _L0_gnn_in['W'], 'L0_gnn_a1': _L0_gnn_in['a1'], 'L0_gnn_a2': _L0_gnn_in['a2'], 'L0_gnn_bias': _L0_gnn_in['bias'], 'L1_gnn_W': _L1_gnn_in['W'], 'L1_gnn_b': _L1_gnn_in['b'], 'L1_gnn_gamma': _L1_gnn_in['gamma'], 'L1_gnn_beta': _L1_gnn_in['beta']}

def reference(x, adj, L0_gnn_W, L0_gnn_a1, L0_gnn_a2, L0_gnn_bias, L1_gnn_W, L1_gnn_b, L1_gnn_gamma, L1_gnn_beta):
    import jax
    import jax.numpy as jnp

    def _L0_gnn_ref(input, adj, W, a1, a2, bias):
        import jax, jax.numpy as jnp
        import numpy as np
        ALPHA = 0.2
        h = jnp.einsum('bnf,fo->bno', input, W)
        f1 = h @ a1
        f2 = h @ a2
        e = f1 + jnp.swapaxes(f2, 1, 2)
        e = jnp.where(e >= 0, e, ALPHA * e)
        attention = jax.nn.softmax(adj * e, axis=1)
        h_prime = jnp.einsum('bij,bjo->bio', attention, h) + bias[None, :, :]
        return h_prime + input

    def _L1_gnn_ref(x, adj, W, b, gamma, beta):
        import jax, jax.numpy as jnp
        import numpy as np
        BN_EPS = 1e-05
        support = jnp.einsum('bnd,df->bnf', x, W) + b
        y = jnp.einsum('bnm,bmf->bnf', adj, support)
        mean = jnp.mean(y, axis=(0, 1))
        var = jnp.mean(jnp.square(y - mean), axis=(0, 1))
        y = (y - mean) * jax.lax.rsqrt(var + BN_EPS) * gamma + beta
        y = jax.nn.relu(y)
        return y + x
    x = _L0_gnn_ref(x, adj, L0_gnn_W, L0_gnn_a1, L0_gnn_a2, L0_gnn_bias)
    x = _L1_gnn_ref(x, adj, L1_gnn_W, L1_gnn_b, L1_gnn_gamma, L1_gnn_beta)
    return x

_drawn_inputs = setup_inputs


def setup_inputs(seed=0):
    import zlib

    import numpy as np

    out = dict(_drawn_inputs(seed))
    spreads = {'L1_gnn_gamma': (1.0, 0.2), 'L1_gnn_beta': (0.0, 0.1)}
    factors = {'L0_gnn_bias': 2.853, 'L1_gnn_b': 8.0}
    for name, (base, spread) in spreads.items():
        noise = np.random.default_rng([zlib.crc32(name.encode()), seed]).standard_normal(out[name].shape)
        drawn = base * np.exp(spread * noise) if base else spread * noise
        out[name] = jnp.asarray(drawn.astype(out[name].dtype))
    for name, factor in factors.items():
        out[name] = (out[name] * factor).astype(out[name].dtype)
    return out
```

```python
from contextlib import ExitStack

import concourse.bass as bass
from concourse import mybir

F32 = mybir.dt.float32
ALU = mybir.AluOpType
ACT = mybir.ActivationFunctionType

ALPHA = 0.2
BN_EPS = 1e-5
P = 128
FA1, FA2, FB2 = range(3)
SCRATCH = 1024


class Batch:

    def __init__(self, n, half, par):
        self.n, self.half, self.par = n, half, par

    def next(self):
        return Batch(self.n + 1, self.half if self.par == 0 else self.half + 1, 1 - self.par)

    def prev(self):
        return Batch(self.n - 1, self.half if self.par == 1 else self.half - 1, 1 - self.par)


def build(nc, adjT, xT, biasT, W, WT, a12, W1, b1, gamma, beta, outT):
    B, F, N = xT.shape
    NT = N // P
    CH = 512
    NC = N // CH
    TC = CH // P
    PRE = 2
    SLOTS = NT + PRE
    ER = 4
    SIGMA = list(range(PRE, NT - 2)) + [1, NT - 2, NT - 1, 0]
    assert F == P and B == 8 and NT == 16 and sorted(SIGMA) == list(range(NT))

    def slot_of(par, t):
        return NT + t if (par and t < PRE) else t

    X_STAGE = {0: slot_of(1, 0), 1: slot_of(1, 1), **{b: NT + 1 - b for b in range(2, B)}}
    STAGED = set(X_STAGE.values())

    with ExitStack() as ctx:
        def sb(name, shape):
            return ctx.enter_context(nc.sbuf_tensor(name, shape, F32))

        def sem(name):
            return ctx.enter_context(nc.semaphore(name))

        f1_rows = nc.dram_tensor("f1_rows", [B, N], F32, kind="Internal").ap()
        xp_dram = nc.dram_tensor("xp_dram", [B, P, N], F32, kind="Internal").ap()
        y_dram = nc.dram_tensor("y_dram", [B, P, N], F32, kind="Internal").ap()

        slots = [sb(f"adj_slot{s}", [P, N]) for s in range(SLOTS)]
        scores = [sb(f"scores{e}", [P, N]) for e in range(ER)]
        f1_all = sb("f1_all", [P, N])
        region = [sb("region_even", [P, N]), sb("region_odd", [P, N])]
        bias_sb = sb("bias_sb", [P, N])
        hz = [sb(f"hz{e}", [P, P]) for e in range(ER)]
        w_sb = sb("w_sb", [P, P])
        w1_sb = sb("w1_sb", [P, P])
        b1_sb = sb("b1_sb", [P, P])
        wt_sb = sb("wt_sb", [P, P])
        a12_sb = sb("a12_sb", [P, 2])
        wa_sb = sb("wa_sb", [P, 3])
        ident = sb("ident", [P, P])
        f12 = sb("f12", [P, B, NT, 3])
        f1_row = sb("f1_row", [NT, P])
        mx = sb("mx", [P, ER])
        neg_mx = sb("neg_mx", [P, ER])
        zsum = sb("zsum", [P, ER])
        rz = sb("rz", [P, ER])
        stats = sb("stats", [P, B, NC, 6])
        mv = sb("mv", [P, 2])
        gb = sb("gb", [P, 2])
        eps = sb("eps", [P, 1])
        bn = sb("bn", [P, 4])
        acc0 = [ctx.enter_context(nc.psum_tensor(f"acc0_{c}", [P, CH], F32)) for c in range(NC)]
        acc1 = [ctx.enter_context(nc.psum_tensor(f"acc1_{c}", [P, CH], F32)) for c in range(NC)]

        slot_loaded = [sem(f"slot_loaded{s}") for s in range(SLOTS)]
        wt_loaded, w_loaded, w1_loaded = sem("wt_loaded"), sem("w_loaded"), sem("w1_loaded")
        a12_loaded, b1_loaded, bias_loaded = sem("a12_loaded"), sem("b1_loaded"), sem("bias_loaded")
        gb_loaded = sem("gb_loaded")
        f1_stored, f1_loaded = sem("f1_stored"), sem("f1_loaded")
        x_loaded = [sem(f"x_loaded{c}") for c in range(NC)]
        xp_stored = [sem(f"xp_stored{c}") for c in range(NC)]
        y_stored = [sem(f"y_stored{c}") for c in range(NC)]
        out_stored = sem("out_stored")
        wa_mm, f_mm, f_turned = sem("wa_mm"), sem("f_mm"), sem("f_turned")
        h_mm, sup_mm = sem("h_mm"), sem("sup_mm")
        l0_tile, l0_chunk = sem("l0_tile"), sem("l0_chunk")
        l1_tile, l1_chunk = sem("l1_tile"), sem("l1_chunk")
        relu_out, exp_done = sem("relu_out"), sem("exp_done")
        h_out, y_out, sqrt_done, relu_done = sem("h_out"), sem("y_out"), sem("sqrt_done"), sem("relu_done")
        wa_out, f_out, row_out = sem("wa_out"), sem("f_out"), sem("row_out")
        leaky_done, score_begun = sem("leaky_done"), sem("score_begun")
        max_done, neg_done, rz_done = sem("max_done"), sem("neg_done"), sem("rz_done")
        xp_done, sup_out, stats_done = sem("xp_done"), sem("sup_out"), sem("stats_done")
        eps_set, mv_done, bn_done, sum_done = sem("eps_set"), sem("mv_done"), sem("bn_done"), sem("sum_done")
        ident_set, hz_done, xb_done = sem("ident_set"), sem("hz_done"), sem("xb_done")

        def cols(c):
            return slice(c * CH, (c + 1) * CH)

        def tile_cols(t):
            return slice(t * P, (t + 1) * P)

        def adj_value(bt, t):
            if t == 0:
                return 16 * (bt.half + 1 + bt.par)
            if t < PRE:
                return 16 * (bt.n + 1)
            return 16 * (bt.n + 1 + (t in STAGED))

        def wait_l0(eng, bt, t):
            if t == NT - 1:
                eng.wait_ge(l0_chunk, NC * (bt.n + 1))
            else:
                eng.wait_ge(l0_tile, (NT - 1) * bt.n + t + 1)

        def wait_l1(eng, bt, k):
            if k == NT - 1:
                eng.wait_ge(l1_chunk, NC * (bt.n + 1))
            else:
                eng.wait_ge(l1_tile, (NT - 1) * bt.n + k + 1)

        def wait_ring(eng, bt, t):
            if t >= ER:
                wait_l0(eng, bt, t - ER)
            elif not is_first(bt):
                wait_l0(eng, bt.prev(), t - ER + NT)

        def is_first(bt):
            return isinstance(bt.n, int) and bt.n == 0

        def is_last(bt):
            return isinstance(bt.n, int) and bt.n == B - 1

        def steps(eng, step):
            step(Batch(0, 0, 0))
            with eng.Fori(0, (B - 2) // 2) as i:
                step(Batch(2 * i + 1, i, 1))
                step(Batch(2 * i + 2, i + 1, 0))
            step(Batch(B - 1, (B - 1) // 2, 1))

        loads = [(y_dram, b, "y") for b in range(B - 1)]
        order = [x for b in range(B - 1) for x in (("y", b), ("xp", b))] + [("xp", B - 1)]
        places = list(range(PRE)) + [slot_of(1, t) for t in SIGMA]
        place = dict(zip(order, places))
        earlier = {s: 0 for s in range(SLOTS)}
        for b in range(B):
            for t in range(NT):
                earlier[slot_of(b % 2, t)] += 1
        for s in STAGED:
            earlier[s] += 1
        for b in range(2, B):
            earlier[slot_of(b % 2, 1)] += 1

        block = ctx.enter_context(nc.Block())

        @block.sync
        def _(sp):
            def load_adj(bt, t):
                s = slot_of(bt.par, t)
                sp.dma_start(slots[s][:, :], adjT[bt.n, tile_cols(t), :]).then_inc(slot_loaded[s], 16)

            def load_x(b, s):
                sp.dma_start(slots[s][:, :], xT[b]).then_inc(slot_loaded[s], 16)

            def load_residual(bt, c):
                sp.wait_ge(hz_done, NT * bt.n + TC * (c + 1))
                sp.dma_start(region[bt.par][:, cols(c)], xT[bt.n][:, cols(c)]).then_inc(x_loaded[c], 16)

            def store_xp(bt):
                for c in range(NC):
                    sp.wait_ge(xp_done, NC * bt.n + c + 1)
                    sp.dma_start(xp_dram[bt.n][:, cols(c)], region[bt.par][:, cols(c)]).then_inc(xp_stored[c], 16)

            def step(bt):
                nx = bt.next()
                if is_first(bt):
                    for k in range(NT):
                        if k + 1 < B:
                            load_x(k + 1, X_STAGE[k + 1])
                        if k + 1 >= NT:
                            continue
                        t = k + 1
                        if t in STAGED:
                            sp.wait_ge(f_mm, NT + 1 - t + 1)
                        load_adj(bt, t)
                    sp.wait_ge(h_mm, NC)
                    load_adj(nx, 0)
                    for c in range(NC):
                        load_residual(bt, c)
                else:
                    pv = bt.prev()
                    for k, t in enumerate(SIGMA):
                        wait_l1(sp, pv, k)
                        if t >= PRE:
                            load_adj(bt, t)
                        elif not is_last(bt):
                            if t == 1:
                                load_x(nx.n, slot_of(nx.par, 1))
                            else:
                                load_adj(nx, 0)
                        if k == 7:
                            load_residual(bt, 0)
                        if k == 11:
                            load_residual(bt, 1)
                        if k == 14:
                            load_residual(bt, 2)
                    load_residual(bt, 3)
                    for c in range(NC):
                        sp.wait_ge(y_out, NC * pv.n + c + 1)
                        sp.dma_start(y_dram[pv.n][:, cols(c)], region[pv.par][:, cols(c)]).then_inc(y_stored[c], 16)
                if not is_last(bt):
                    sp.wait_ge(h_mm, NC * (nx.n + 1))
                    load_adj(nx, 1)
                store_xp(bt)

            sp.dma_start(wt_sb[:, :], WT).then_inc(wt_loaded, 16)
            sp.dma_start(a12_sb[:, :], a12).then_inc(a12_loaded, 16)
            load_x(0, X_STAGE[0])
            sp.dma_start(w_sb[:, :], W).then_inc(w_loaded, 16)
            load_adj(Batch(0, 0, 0), 0)
            sp.dma_start(w1_sb[:, :], W1).then_inc(w1_loaded, 16)
            sp.dma_start(b1_sb[:, :], b1.partition_broadcast(P)).then_inc(b1_loaded, 16)
            sp.dma_start(bias_sb[:, :], biasT).then_inc(bias_loaded, 16)
            sp.dma_start(gb[:, 0:1], gamma).then_inc(gb_loaded, 16)
            sp.dma_start(gb[:, 1:2], beta).then_inc(gb_loaded, 16)
            steps(sp, step)

            for c in range(NC):
                sp.wait_ge(y_stored[c], 16 * (B - 1))
                sp.wait_ge(xp_stored[c], 16 * B)
            for n, (what, b) in enumerate(order):
                if n >= PRE:
                    wait_l1(sp, Batch(B - 1, (B - 1) // 2, 1), n - PRE)
                s = place[what, b]
                src = y_dram if what == "y" else xp_dram
                sp.dma_start(slots[s][:, :], src[b]).then_inc(slot_loaded[s], 16)
            for b in [B - 1, *range(B - 1)]:
                n = 0 if b == B - 1 else b + 1
                sp.wait_ge(sum_done, n + 1)
                sp.dma_start(outT[b], slots[place["xp", b]][:, :]).then_inc(out_stored, 16)
            sp.wait_ge(out_stored, 16 * B)

        @block.tensor
        def _(pe):
            def f_columns(b):
                pe.wait_ge(slot_loaded[X_STAGE[b]], 16)
                if b == 0:
                    pe.wait_ge(wa_out, 2)
                else:
                    pe.wait_ge(f_out, b)
                for t in range(NT):
                    mm = pe.matmul(acc1[0][:, 3 * t:3 * t + 3], slots[X_STAGE[b]][:, tile_cols(t)], wa_sb[:, :],
                                   start=True, stop=True)
                mm.then_inc(f_mm, 1)

            def turn_f1(b):
                pe.wait_ge(f_out, b + 1)
                if b == 0:
                    pe.wait_ge(ident_set, 2)
                else:
                    pe.wait_ge(row_out, b)
                pe.transpose(acc1[1][0:NT, 0:P], f12[:, b, :, FA1], ident[:, :]).then_inc(f_turned, 1)

            def make_h(bt, x, banks):
                for c in range(NC):
                    if not isinstance(bt.n, int) or bt.n >= 2:
                        pe.wait_ge(y_out, NC * (bt.n - 2) + c + 1)
                    for q in range(TC):
                        mm = pe.matmul(banks[c][:, tile_cols(q)], x[:, tile_cols(TC * c + q)], w_sb[:, :],
                                       start=True, stop=True)
                    mm.then_inc(h_mm, 1)

            def layer0(bt, t, support=False):
                e = t % ER
                pe.wait_ge(exp_done, NT * bt.n + t + 1)
                pe.wait_ge(hz_done, NT * bt.n + t + 1)
                for c in range(NC):
                    if t == 0 and is_first(bt):
                        pe.wait_ge(h_out, c + 1)
                    elif t == 0:
                        pe.wait_ge(sup_out, NC * (bt.n - 1) + c + 1)
                    mm = pe.matmul(acc0[c][:, :], hz[e][:, :], scores[e][:, cols(c)],
                                   start=(t == 0), stop=(t == NT - 1))
                    if t == NT - 1:
                        mm.then_inc(l0_chunk, 1)
                        if c >= 2:
                            make_support(bt, c - 2)
                if t < NT - 1:
                    mm.then_inc(l0_tile, 1)
                else:
                    for c in range(NC - 2, NC):
                        make_support(bt, c)

            def make_support(bt, c):
                pe.wait_ge(xp_done, NC * bt.n + c + 1)
                for q in range(TC):
                    mm = pe.matmul(acc0[c][:, tile_cols(q)], region[bt.par][:, tile_cols(TC * c + q)], w1_sb[:, :],
                                   start=True, stop=True)
                mm.then_inc(sup_mm, 1)

            def layer1(bt, k, last=False):
                t = SIGMA[k]
                if k == 0 or t % TC == 0:
                    pe.wait_ge(sup_out, NC * bt.n + t // TC + 1)
                for c in range(NC):
                    if k == 0 and not last:
                        pe.wait_ge(h_out, NC * (bt.n + 1) + c + 1)
                    elif k == 0:
                        pe.wait_ge(y_out, NC * (bt.n - 1) + c + 1)
                    mm = pe.matmul(acc1[c][:, :], region[bt.par][:, tile_cols(t)],
                                   slots[slot_of(bt.par, t)][:, cols(c)], start=(k == 0), stop=(k == NT - 1))
                    if k == NT - 1:
                        mm.then_inc(l1_chunk, 1)
                if k < NT - 1:
                    mm.then_inc(l1_tile, 1)

            def step(bt):
                nx = bt.next()
                ahead = 0
                for t in range(NT):
                    if is_first(bt):
                        if t + 1 < B:
                            f_columns(t + 1)
                    else:
                        while ahead < min(t + 2 if t >= 2 else t + 1, NT):
                            layer1(bt.prev(), ahead)
                            ahead += 1
                    if t == NT - 1 and not is_last(bt):
                        if is_first(bt):
                            pe.wait_ge(f_out, B)
                            pe.wait_ge(row_out, B)
                            pe.wait_ge(slot_loaded[X_STAGE[1]], 16)
                        else:
                            pe.wait_ge(slot_loaded[slot_of(nx.par, 1)], 16 * nx.n)
                        make_h(nx, slots[slot_of(nx.par, 1)], acc1)
                    layer0(bt, t)
                    if is_first(bt) and t + 1 < B:
                        turn_f1(t + 1)

            pe.wait_ge(wt_loaded, 16)
            pe.wait_ge(a12_loaded, 16)
            pe.matmul(acc1[2][:, 0:2], wt_sb[:, :], a12_sb[:, :], start=True, stop=True).then_inc(wa_mm, 1)
            f_columns(0)
            turn_f1(0)
            pe.wait_ge(w_loaded, 16)
            make_h(Batch(0, 0, 0), slots[X_STAGE[0]], acc0)
            pe.wait_ge(w1_loaded, 16)
            steps(pe, step)
            for k in range(NT):
                layer1(Batch(B - 1, (B - 1) // 2, 1), k, last=True)

        @block.scalar
        def _(act):
            def store_f1(b):
                act.wait_ge(row_out, b + 1)
                act.dma_start(f1_rows[b].rearrange("(t p) -> t p", p=P), f1_row[:, :]).then_inc(f1_stored, 16)

            def load_f1(bt):
                act.wait_ge(f1_stored, 16 * B if not is_first(bt) else 16)
                act.dma_start(f1_all[:, :], f1_rows[bt.n].partition_broadcast(P)).then_inc(f1_loaded, 16)

            def positive_part(bt, t):
                if t == 0:
                    act.wait_ge(f1_loaded, 16 * (bt.n + 1))
                if t == 0 and is_first(bt):
                    act.wait_ge(f_out, 1)
                wait_ring(act, bt, t)
                act.activation(scores[t % ER][:, :], f1_all[:, :], ACT.Relu, scale=(1 - ALPHA) / ALPHA,
                               bias=f12[:, bt.n, t, FB2:FB2 + 1]).then_inc(relu_out, 1)

            def exp(bt, t):
                e = t % ER
                act.wait_ge(neg_done, NT * bt.n + t + 1)
                act.activation(scores[e][:, :], scores[e][:, :], ACT.Exp, bias=neg_mx[:, e:e + 1],
                               accum_out=zsum[:, e:e + 1]).then_inc(exp_done, 1)

            def h_from_psum(bt, banks):
                for c in range(NC):
                    act.wait_ge(h_mm, NC * bt.n + c + 1)
                    if not isinstance(bt.n, int) or bt.n >= 2:
                        act.wait_ge(y_stored[c], 16 * (bt.n - 1))
                        act.wait_ge(stats_done, NC * (bt.n - 2) + c + 1)
                    act.copy(region[bt.par][:, cols(c)], banks[c][:, :]).then_inc(h_out, 1)

            def y_from_psum(bt):
                wait_l1(act, bt, NT - 1)
                for c in range(NC):
                    act.copy(region[bt.par][:, cols(c)], acc1[c][:, :]).then_inc(y_out, 1)

            def step(bt):
                nx = bt.next()
                for t in range(NT):
                    exp(bt, t)
                    if t + 2 < NT:
                        positive_part(bt, t + 2)
                    if is_first(bt) and 1 <= t < B:
                        store_f1(t)
                if not is_last(bt):
                    act.wait_ge(leaky_done, NT * nx.n)
                    load_f1(nx)
                    positive_part(nx, 0)
                    positive_part(nx, 1)
                if not is_first(bt):
                    y_from_psum(bt.prev())
                if not is_last(bt):
                    h_from_psum(nx, acc1)

            first = Batch(0, 0, 0)
            store_f1(0)
            load_f1(first)
            h_from_psum(first, acc0)
            positive_part(first, 0)
            positive_part(first, 1)
            steps(act, step)
            y_from_psum(Batch(B - 1, (B - 1) // 2, 1))

            act.wait_ge(mv_done, 1)
            act.wait_ge(eps_set, 1)
            act.activation(bn[:, 0:1], mv[:, 1:2], ACT.Sqrt, bias=eps[:, 0:1]).then_inc(sqrt_done, 1)
            act.wait_ge(bn_done, 4)
            for b in [B - 1, *range(B - 1)]:
                if b == B - 1:
                    y = region[b % 2]
                else:
                    s = place["y", b]
                    act.wait_ge(slot_loaded[s], 16 * (earlier[s] + 1))
                    y = slots[s]
                act.activation(y[:, :], y[:, :], ACT.Relu, scale=bn[:, 2:3], bias=bn[:, 3:4]).then_inc(relu_done, 1)

        @block.vector
        def _(dve):
            def f_from_psum(b):
                dve.wait_ge(f_mm, b + 1)
                dve.tensor_copy(f12[:, b, :, :], acc1[0][:, 0:3 * NT]).then_inc(f_out, 1)

            def row_from_psum(b):
                dve.wait_ge(f_turned, b + 1)
                if b:
                    dve.wait_ge(f1_stored, 16 * b)
                dve.tensor_copy(f1_row[:, :], acc1[1][0:NT, 0:P]).then_inc(row_out, 1)

            def score(bt, t):
                e, s = t % ER, slot_of(bt.par, t)
                dve.wait_ge(relu_out, NT * bt.n + t + 1)
                dve.scalar_tensor_tensor(out=scores[e][:, :], in0=scores[e][:, :], scalar=f12[:, bt.n, t, FA2:FA2 + 1],
                                         in1=f1_all[:, :], op0=ALU.add, op1=ALU.add).then_inc(leaky_done, 1)
                dve.wait_ge(leaky_done, NT * bt.n + t + 1)
                dve.wait_ge(slot_loaded[s], adj_value(bt, t))
                dve.sem_inc(score_begun, 1)
                dve.tensor_tensor_reduce(scores[e][:, :], scores[e][:, :], slots[s][:, :], 1.0, NEG_BIG,
                                         ALU.mult, ALU.max, mx[:, e:e + 1]).then_inc(max_done, 1)
                dve.wait_ge(max_done, NT * bt.n + t + 1)
                dve.tensor_scalar(neg_mx[:, e:e + 1], mx[:, e:e + 1], -1.0, None, ALU.mult).then_inc(neg_done, 1)

            def recip(bt, t):
                e = t % ER
                dve.wait_ge(exp_done, NT * bt.n + t + 1)
                wait_hz(bt, t)
                dve.reciprocal(rz[:, e:e + 1], zsum[:, e:e + 1]).then_inc(rz_done, 1)

            def wait_hz(bt, t):
                if not (is_first(bt) and t < ER):
                    dve.wait_ge(hz_done, NT * bt.n + t - ER + 1)

            def y_stats(bt):
                for c in range(NC):
                    dve.wait_ge(y_out, NC * bt.n + c + 1)
                    dve.bn_stats(stats[:, bt.n, c, :], region[bt.par][:, cols(c)]).then_inc(stats_done, 1)

            def make_xp(bt, c):
                dve.wait_ge(l0_chunk, NC * bt.n + c + 1)
                dve.wait_ge(xb_done, NC * bt.n + c + 1)
                dve.tensor_tensor(region[bt.par][:, cols(c)], acc0[c][:, :], region[bt.par][:, cols(c)],
                                  ALU.add).then_inc(xp_done, 1)

            def support_from_psum(bt, c):
                dve.wait_ge(sup_mm, NC * bt.n + c + 1)
                dve.wait_ge(xp_stored[c], 16 * (bt.n + 1))
                dve.tensor_tensor(region[bt.par][:, cols(c)].rearrange("p (t f) -> p t f", f=P),
                                  acc0[c][:, :].rearrange("p (t f) -> p t f", f=P),
                                  b1_sb[:, :].unsqueeze(1).to_broadcast([P, TC, P]), ALU.add).then_inc(sup_out, 1)

            def step(bt):
                nx = bt.next()
                for t in range(NT):
                    if t > 0 or is_first(bt):
                        score(bt, t)
                    if t > 0:
                        recip(bt, t - 1)
                    if is_first(bt) and t + 1 < B:
                        f_from_psum(t + 1)
                    if is_first(bt) and 1 <= t < B:
                        row_from_psum(t)
                recip(bt, NT - 1)
                if not is_first(bt):
                    y_stats(bt.prev())
                if not is_last(bt):
                    score(nx, 0)
                for c in range(NC + 1):
                    if c < NC:
                        make_xp(bt, c)
                    if c > 0:
                        support_from_psum(bt, c - 1)

            dve.memset(eps[:, :], BN_EPS).then_inc(eps_set, 1)
            dve.wait_ge(wa_mm, 1)
            dve.tensor_scalar(wa_sb[:, FA1:FA2 + 1], acc1[2][:, 0:2], ALPHA, None, ALU.mult).then_inc(wa_out, 1)
            dve.tensor_scalar(wa_sb[:, FB2:FB2 + 1], acc1[2][:, 1:2], 1 - ALPHA, None, ALU.mult).then_inc(wa_out, 1)
            f_from_psum(0)
            row_from_psum(0)
            dve.wait_ge(b1_loaded, 16)
            steps(dve, step)
            y_stats(Batch(B - 1, (B - 1) // 2, 1))

            dve.wait_ge(stats_done, NC * B)
            dve.bn_aggr(mv[:, :], stats[:, :, :, :].rearrange("p b c s -> p (b c s)")).then_inc(mv_done, 1)
            dve.wait_ge(gb_loaded, 32)
            dve.wait_ge(sqrt_done, 1)
            dve.reciprocal(bn[:, 1:2], bn[:, 0:1]).then_inc(bn_done, 1)
            dve.wait_ge(bn_done, 1)
            dve.tensor_tensor(bn[:, 2:3], gb[:, 0:1], bn[:, 1:2], ALU.mult).then_inc(bn_done, 1)
            dve.wait_ge(bn_done, 2)
            dve.tensor_tensor(bn[:, 0:1], mv[:, 0:1], bn[:, 2:3], ALU.mult).then_inc(bn_done, 1)
            dve.wait_ge(bn_done, 3)
            dve.tensor_tensor(bn[:, 3:4], gb[:, 1:2], bn[:, 0:1], ALU.subtract).then_inc(bn_done, 1)
            for n, b in enumerate([B - 1, *range(B - 1)]):
                s = place["xp", b]
                y = region[b % 2] if b == B - 1 else slots[place["y", b]]
                dve.wait_ge(slot_loaded[s], 16 * (earlier[s] + 1))
                dve.wait_ge(relu_done, n + 1)
                dve.tensor_tensor(slots[s][:, :], slots[s][:, :], y[:, :], ALU.add).then_inc(sum_done, 1)

        @block.gpsimd
        def _(pool):
            def scale_h(bt, t):
                e = t % ER
                pool.wait_ge(rz_done, NT * bt.n + t + 1)
                if t % TC == 0:
                    pool.wait_ge(h_out, NC * bt.n + t // TC + 1)
                wait_ring(pool, bt, t)
                pool.tensor_tensor(hz[e][:, :], region[bt.par][:, tile_cols(t)],
                                   rz[:, e:e + 1].to_broadcast([P, P]), ALU.mult).then_inc(hz_done, 1)

            def add_bias(bt, c):
                pool.wait_ge(x_loaded[c], 16 * (bt.n + 1))
                pool.tensor_tensor(region[bt.par][:, cols(c)], region[bt.par][:, cols(c)],
                                   bias_sb[:, cols(c)], ALU.add).then_inc(xb_done, 1)

            def step(bt):
                for t in range(NT):
                    scale_h(bt, t)
                    if t == NT - 4 and not is_first(bt):
                        add_bias(bt, 0)
                for c in range(0 if is_first(bt) else 1, NC):
                    add_bias(bt, c)

            pool.memset(ident[:, :], 0.0).then_inc(ident_set, 1)
            pool.wait_ge(ident_set, 1)
            pool.affine_select(out=ident[:, :], in_=ident[:, :], compare_op=ALU.not_equal, fill=1.0,
                               base=0, pattern=[[-1, P]], channel_multiplier=1).then_inc(ident_set, 1)
            pool.wait_ge(bias_loaded, 16)
            steps(pool, step)


NEG_BIG = -3.4028234663852886e38


def kernel(x, adj, L0_gnn_W, L0_gnn_a1, L0_gnn_a2, L0_gnn_bias, L1_gnn_W, L1_gnn_b, L1_gnn_gamma, L1_gnn_beta):
    import numpy as np
    import concourse.bacc as bacc
    from concourse.bass_utils import run_bass_kernel_spmd

    def lay(a):
        return np.ascontiguousarray(a)

    x, adj, W = np.asarray(x), np.asarray(adj), np.asarray(L0_gnn_W)
    arrays = {
        "adjT": lay(adj.transpose(0, 2, 1)),
        "xT": lay(x.transpose(0, 2, 1)),
        "biasT": lay(np.asarray(L0_gnn_bias).T),
        "W": lay(W),
        "WT": lay(W.T),
        "a12": lay(np.concatenate([np.asarray(L0_gnn_a1), np.asarray(L0_gnn_a2)], axis=1)),
        "W1": lay(L1_gnn_W),
        "b1": lay(L1_gnn_b),
        "gamma": lay(np.asarray(L1_gnn_gamma).reshape(-1, 1)),
        "beta": lay(np.asarray(L1_gnn_beta).reshape(-1, 1)),
    }
    nc = bacc.Bacc("TRN2", target_bir_lowering=False, num_devices=1, dynamic_dma_scratch_size=SCRATCH)
    args = [nc.dram_tensor(name, a.shape, F32, kind="ExternalInput").ap() for name, a in arrays.items()]
    out = nc.dram_tensor("outT", arrays["xT"].shape, F32, kind="ExternalOutput").ap()
    build(nc, *args, out)
    r = run_bass_kernel_spmd(nc, [arrays], core_ids=[0])
    return np.ascontiguousarray(np.asarray(r.results[0]["outT"]).transpose(0, 2, 1))
```

```python
from contextlib import ExitStack

import concourse.bass as bass
from concourse import mybir

F32 = mybir.dt.float32
ALU = mybir.AluOpType
ACT = mybir.ActivationFunctionType

ALPHA = 0.2
BN_EPS = 1e-5
P = 128
FA1, FA2, FB2 = range(3)
SCRATCH = 1024


class Batch:

    def __init__(self, n, half, par):
        self.n, self.half, self.par = n, half, par

    def next(self):
        return Batch(self.n + 1, self.half if self.par == 0 else self.half + 1, 1 - self.par)

    def prev(self):
        return Batch(self.n - 1, self.half if self.par == 1 else self.half - 1, 1 - self.par)


def build(nc, adjT, xT, biasT, W, WT, a12, W1, b1, gamma, beta, outT):
    B, F, N = xT.shape
    NT = N // P
    CH = 512
    NC = N // CH
    TC = CH // P
    PRE = 2
    SLOTS = NT + PRE
    ER = 4
    SIGMA = list(range(PRE, NT - 2)) + [1, NT - 2, NT - 1, 0]
    assert F == P and B == 8 and NT == 16 and sorted(SIGMA) == list(range(NT))

    def slot_of(par, t):
        return NT + t if (par and t < PRE) else t

    X_STAGE = {0: slot_of(1, 0), 1: slot_of(1, 1), **{b: NT + 1 - b for b in range(2, B)}}
    STAGED = set(X_STAGE.values())

    with ExitStack() as ctx:
        def sb(name, shape):
            return ctx.enter_context(nc.sbuf_tensor(name, shape, F32))

        def sem(name):
            return ctx.enter_context(nc.semaphore(name))

        f1_rows = nc.dram_tensor("f1_rows", [B, N], F32, kind="Internal").ap()
        xp_dram = nc.dram_tensor("xp_dram", [B, P, N], F32, kind="Internal").ap()
        y_dram = nc.dram_tensor("y_dram", [B, P, N], F32, kind="Internal").ap()

        slots = [sb(f"adj_slot{s}", [P, N]) for s in range(SLOTS)]
        scores = [sb(f"scores{e}", [P, N]) for e in range(ER)]
        f1_all = [sb("f1_even", [P, N]), sb("f1_odd", [P, N])]
        region = [sb("region_even", [P, N]), sb("region_odd", [P, N])]
        bias_sb = sb("bias_sb", [P, N])
        hz = [sb(f"hz{e}", [P, P]) for e in range(ER)]
        w_sb = sb("w_sb", [P, P])
        w1_sb = sb("w1_sb", [P, P])
        b1_sb = sb("b1_sb", [P, P])
        a12_sb = sb("a12_sb", [P, 2])
        wa_sb = sb("wa_sb", [P, 3])
        f12 = sb("f12", [P, B, NT, 3])
        mx = sb("mx", [P, ER])
        neg_mx = sb("neg_mx", [P, ER])
        zsum = sb("zsum", [P, ER])
        rz = sb("rz", [P, ER])
        stats = sb("stats", [P, B, NC, 6])
        mv = sb("mv", [P, 2])
        gb = sb("gb", [P, 2])
        eps = sb("eps", [P, 1])
        bn = sb("bn", [P, 4])
        wt_sb = scores[ER - 1][:, 0:P]
        ident = region[1][:, 0:P]
        f1_row = region[1][0:NT, P:2 * P]
        wa1_cols = region[1][:, 2 * P:3 * P]
        acc0 = [ctx.enter_context(nc.psum_tensor(f"acc0_{c}", [P, CH], F32)) for c in range(NC)]
        acc1 = [ctx.enter_context(nc.psum_tensor(f"acc1_{c}", [P, CH], F32)) for c in range(NC)]

        slot_loaded = [sem(f"slot_loaded{s}") for s in range(SLOTS)]
        wt_loaded, w_loaded, w1_loaded = sem("wt_loaded"), sem("w_loaded"), sem("w1_loaded")
        a12_loaded, b1_loaded, bias_loaded = sem("a12_loaded"), sem("b1_loaded"), sem("bias_loaded")
        gb_loaded = sem("gb_loaded")
        f1_stored, f1_loaded = sem("f1_stored"), [sem("f1_loaded_even"), sem("f1_loaded_odd")]
        x_loaded = [sem(f"x_loaded{c}") for c in range(NC)]
        xp_stored = [sem(f"xp_stored{c}") for c in range(NC)]
        y_stored = [sem(f"y_stored{c}") for c in range(NC)]
        out_stored = sem("out_stored")
        wa_mm, f1_mm, f_mm, f_turned = sem("wa_mm"), sem("f1_mm"), sem("f_mm"), sem("f_turned")
        h_mm, sup_mm = sem("h_mm"), sem("sup_mm")
        l0_tile, l0_chunk = sem("l0_tile"), sem("l0_chunk")
        l1_tile, l1_chunk = sem("l1_tile"), sem("l1_chunk")
        f1_out = sem("f1_out")
        relu_out, exp_done = sem("relu_out"), sem("exp_done")
        h_out, y_out, sqrt_done, relu_done = sem("h_out"), sem("y_out"), sem("sqrt_done"), sem("relu_done")
        wa_out, f_out, row_out = sem("wa_out"), sem("f_out"), sem("row_out")
        leaky_done, score_begun = sem("leaky_done"), sem("score_begun")
        max_done, neg_done, rz_done = sem("max_done"), sem("neg_done"), sem("rz_done")
        xp_done, sup_out, stats_done = sem("xp_done"), sem("sup_out"), sem("stats_done")
        eps_set, mv_done, bn_done, sum_done = sem("eps_set"), sem("mv_done"), sem("bn_done"), sem("sum_done")
        ident_set, hz_done, xb_done = sem("ident_set"), sem("hz_done"), sem("xb_done")

        def cols(c):
            return slice(c * CH, (c + 1) * CH)

        def tile_cols(t):
            return slice(t * P, (t + 1) * P)

        def adj_value(bt, t):
            if t == 0:
                return 16 * (bt.half + 1 + bt.par)
            if t < PRE:
                return 16 * (bt.n + 1)
            return 16 * (bt.n + 1 + (t in STAGED))

        def wait_l0(eng, bt, t):
            if t == NT - 1:
                eng.wait_ge(l0_chunk, NC * (bt.n + 1))
            else:
                eng.wait_ge(l0_tile, (NT - 1) * bt.n + t + 1)

        def wait_l1(eng, bt, k):
            if k == NT - 1:
                eng.wait_ge(l1_chunk, NC * (bt.n + 1))
            else:
                eng.wait_ge(l1_tile, (NT - 1) * bt.n + k + 1)

        def wait_ring(eng, bt, t):
            if t >= ER:
                wait_l0(eng, bt, t - ER)
            elif not is_first(bt):
                wait_l0(eng, bt.prev(), t - ER + NT)

        def is_first(bt):
            return isinstance(bt.n, int) and bt.n == 0

        def is_last(bt):
            return isinstance(bt.n, int) and bt.n == B - 1

        def steps(eng, step):
            step(Batch(0, 0, 0))
            with eng.Fori(0, (B - 2) // 2) as i:
                step(Batch(2 * i + 1, i, 1))
                step(Batch(2 * i + 2, i + 1, 0))
            step(Batch(B - 1, (B - 1) // 2, 1))

        loads = [(y_dram, b, "y") for b in range(B - 1)]
        order = [x for b in range(B - 1) for x in (("y", b), ("xp", b))] + [("xp", B - 1)]
        places = list(range(PRE)) + [slot_of(1, t) for t in SIGMA]
        place = dict(zip(order, places))
        earlier = {s: 0 for s in range(SLOTS)}
        for b in range(B):
            for t in range(NT):
                earlier[slot_of(b % 2, t)] += 1
        for s in STAGED:
            earlier[s] += 1
        for b in range(2, B):
            earlier[slot_of(b % 2, 1)] += 1

        block = ctx.enter_context(nc.Block())

        @block.sync
        def _(sp):
            def load_adj(bt, t):
                s = slot_of(bt.par, t)
                sp.dma_start(slots[s][:, :], adjT[bt.n, tile_cols(t), :]).then_inc(slot_loaded[s], 16)

            def load_x(b, s):
                sp.dma_start(slots[s][:, :], xT[b]).then_inc(slot_loaded[s], 16)

            def load_residual(bt, c):
                sp.wait_ge(hz_done, NT * bt.n + TC * (c + 1))
                sp.dma_start(region[bt.par][:, cols(c)], xT[bt.n][:, cols(c)]).then_inc(x_loaded[c], 16)

            def store_xp(bt):
                for c in range(NC):
                    sp.wait_ge(xp_done, NC * bt.n + c + 1)
                    sp.dma_start(xp_dram[bt.n][:, cols(c)], region[bt.par][:, cols(c)]).then_inc(xp_stored[c], 16)

            def step(bt):
                nx = bt.next()
                if is_first(bt):
                    for k in range(NT):
                        if k + 1 >= NT:
                            continue
                        t = k + 1
                        if t > 2:
                            sp.wait_ge(relu_out, t - 1)
                        if t < B:
                            load_x(t, X_STAGE[t])
                        if t in STAGED:
                            sp.wait_ge(f_mm, NT + 1 - t + 1)
                        load_adj(bt, t)
                    sp.dma_start(bias_sb[:, :], biasT).then_inc(bias_loaded, 16)
                    sp.wait_ge(h_mm, NC)
                    load_adj(nx, 0)
                    for c in range(NC):
                        load_residual(bt, c)
                else:
                    pv = bt.prev()
                    for k, t in enumerate(SIGMA):
                        wait_l1(sp, pv, k)
                        if t >= PRE:
                            load_adj(bt, t)
                        elif not is_last(bt):
                            if t == 1:
                                load_x(nx.n, slot_of(nx.par, 1))
                            else:
                                load_adj(nx, 0)
                        if k == 7:
                            load_residual(bt, 0)
                        if k == 11:
                            load_residual(bt, 1)
                        if k == 14:
                            load_residual(bt, 2)
                    load_residual(bt, 3)
                    for c in range(NC):
                        sp.wait_ge(y_out, NC * pv.n + c + 1)
                        sp.dma_start(y_dram[pv.n][:, cols(c)], region[pv.par][:, cols(c)]).then_inc(y_stored[c], 16)
                store_xp(bt)
                if not is_last(bt):
                    sp.wait_ge(h_mm, NC * (nx.n + 1))
                    load_adj(nx, 1)

            sp.dma_start(wt_sb[:, :], WT).then_inc(wt_loaded, 16)
            sp.dma_start(a12_sb[:, :], a12).then_inc(a12_loaded, 16)
            load_x(0, X_STAGE[0])
            sp.dma_start(w_sb[:, :], W).then_inc(w_loaded, 16)
            load_adj(Batch(0, 0, 0), 0)
            sp.dma_start(w1_sb[:, :], W1).then_inc(w1_loaded, 16)
            sp.dma_start(b1_sb[:, :], b1.partition_broadcast(P)).then_inc(b1_loaded, 16)
            sp.dma_start(gb[:, 0:1], gamma).then_inc(gb_loaded, 16)
            sp.dma_start(gb[:, 1:2], beta).then_inc(gb_loaded, 16)
            steps(sp, step)

            for c in range(NC):
                sp.wait_ge(y_stored[c], 16 * (B - 1))
                sp.wait_ge(xp_stored[c], 16 * B)
            for n, (what, b) in enumerate(order):
                if n >= PRE:
                    wait_l1(sp, Batch(B - 1, (B - 1) // 2, 1), n - PRE)
                s = place[what, b]
                src = y_dram if what == "y" else xp_dram
                sp.dma_start(slots[s][:, :], src[b]).then_inc(slot_loaded[s], 16)
            for b in [B - 1, *range(B - 1)]:
                n = 0 if b == B - 1 else b + 1
                sp.wait_ge(sum_done, n + 1)
                sp.dma_start(outT[b], slots[place["xp", b]][:, :]).then_inc(out_stored, 16)
            sp.wait_ge(out_stored, 16 * B)

        @block.tensor
        def _(pe):
            def f_columns(b):
                pe.wait_ge(slot_loaded[X_STAGE[b]], 16)
                if b > 0:
                    pe.wait_ge(f_out, b)
                for t in range(NT):
                    mm = pe.matmul(acc1[0][:, 3 * t:3 * t + 3], slots[X_STAGE[b]][:, tile_cols(t)], wa_sb[:, :],
                                   start=True, stop=True)
                mm.then_inc(f_mm, 1)

            def turn_f1(b):
                pe.wait_ge(f_out, b + 1)
                if b == 1:
                    pe.wait_ge(ident_set, 2)
                else:
                    pe.wait_ge(row_out, b - 1)
                pe.transpose(acc1[1][0:NT, 0:P], f12[:, b, :, FA1], ident[:, :]).then_inc(f_turned, 1)

            def make_h(bt, x, banks, c):
                if not isinstance(bt.n, int) or bt.n >= 2:
                    pe.wait_ge(y_out, NC * (bt.n - 2) + c + 1)
                for q in range(TC):
                    mm = pe.matmul(banks[c][:, tile_cols(q)], x[:, tile_cols(TC * c + q)], w_sb[:, :],
                                   start=True, stop=True)
                mm.then_inc(h_mm, 1)

            def layer0(bt, t):
                e = t % ER
                pe.wait_ge(exp_done, NT * bt.n + t + 1)
                pe.wait_ge(hz_done, NT * bt.n + t + 1)
                for c in range(NC):
                    if t == 0 and is_first(bt):
                        pe.wait_ge(h_out, c + 1)
                    elif t == 0:
                        pe.wait_ge(sup_out, NC * (bt.n - 1) + c + 1)
                    mm = pe.matmul(acc0[c][:, :], hz[e][:, :], scores[e][:, cols(c)],
                                   start=(t == 0), stop=(t == NT - 1))
                    if t == NT - 1:
                        mm.then_inc(l0_chunk, 1)
                if t < NT - 1:
                    mm.then_inc(l0_tile, 1)

            def make_support(bt, c):
                pe.wait_ge(xp_done, NC * bt.n + c + 1)
                for q in range(TC):
                    mm = pe.matmul(acc0[c][:, tile_cols(q)], region[bt.par][:, tile_cols(TC * c + q)], w1_sb[:, :],
                                   start=True, stop=True)
                mm.then_inc(sup_mm, 1)

            def layer1(bt, k, last=False):
                t = SIGMA[k]
                if k == 0 or t % TC == 0:
                    pe.wait_ge(sup_out, NC * bt.n + t // TC + 1)
                for c in range(NC):
                    if k == 0 and not last:
                        pe.wait_ge(h_out, NC * (bt.n + 1) + c + 1)
                    elif k == 0:
                        pe.wait_ge(y_out, NC * (bt.n - 1) + c + 1)
                    mm = pe.matmul(acc1[c][:, :], region[bt.par][:, tile_cols(t)],
                                   slots[slot_of(bt.par, t)][:, cols(c)], start=(k == 0), stop=(k == NT - 1))
                    if k == NT - 1:
                        mm.then_inc(l1_chunk, 1)
                if k < NT - 1:
                    mm.then_inc(l1_tile, 1)

            def step(bt):
                nx = bt.next()
                ahead = 0
                for t in range(NT):
                    if is_first(bt):
                        if t + 1 < B:
                            f_columns(t + 1)
                    else:
                        while ahead < min(t + 2 if t >= 2 else t + 1, NT):
                            layer1(bt.prev(), ahead)
                            ahead += 1
                    layer0(bt, t)
                    if is_first(bt) and 2 <= t < B + 1:
                        turn_f1(t - 1)
                if is_first(bt):
                    pe.wait_ge(f_out, B)
                    pe.wait_ge(row_out, B - 1)
                    pe.wait_ge(slot_loaded[X_STAGE[1]], 16)
                elif not is_last(bt):
                    pe.wait_ge(slot_loaded[slot_of(nx.par, 1)], 16 * nx.n)
                for c in range(NC):
                    if not is_last(bt):
                        make_h(nx, slots[slot_of(nx.par, 1)], acc1, c)
                    make_support(bt, c)

            pe.wait_ge(wt_loaded, 16)
            pe.wait_ge(a12_loaded, 16)
            pe.matmul(acc1[2][:, 0:2], wt_sb, a12_sb[:, :], start=True, stop=True).then_inc(wa_mm, 1)
            pe.wait_ge(slot_loaded[X_STAGE[0]], 16)
            pe.wait_ge(wa_out, 3)
            for c in range(NC):
                pe.matmul(acc0[c][:, :], wa1_cols, slots[X_STAGE[0]][:, cols(c)], start=True, stop=True)\
                    .then_inc(f1_mm, 1)
            f_columns(0)
            pe.wait_ge(w_loaded, 16)
            for c in range(NC):
                pe.wait_ge(f1_out, c + 1)
                make_h(Batch(0, 0, 0), slots[X_STAGE[0]], acc0, c)
            pe.wait_ge(w1_loaded, 16)
            steps(pe, step)
            for k in range(NT):
                layer1(Batch(B - 1, (B - 1) // 2, 1), k, last=True)

        @block.scalar
        def _(act):
            def store_f1(b):
                act.wait_ge(row_out, b)
                act.dma_start(f1_rows[b].rearrange("(t p) -> t p", p=P), f1_row[:, :]).then_inc(f1_stored, 16)

            def load_f1(bt):
                if bt.par:
                    act.wait_ge(f1_stored, 16 * (B - 1))
                act.dma_start(f1_all[bt.par][:, :], f1_rows[bt.n].partition_broadcast(P)).then_inc(f1_loaded[bt.par], 16)

            def positive_part(bt, t):
                if t == 0 and not is_first(bt):
                    act.wait_ge(f1_loaded[bt.par], 16 * (bt.half + bt.par))
                if t == 0 and is_first(bt):
                    act.wait_ge(f_out, 1)
                wait_ring(act, bt, t)
                act.activation(scores[t % ER][:, :], f1_all[bt.par][:, :], ACT.Relu, scale=(1 - ALPHA) / ALPHA,
                               bias=f12[:, bt.n, t, FB2:FB2 + 1]).then_inc(relu_out, 1)

            def exp(bt, t):
                e = t % ER
                act.wait_ge(neg_done, NT * bt.n + t + 1)
                act.activation(scores[e][:, :], scores[e][:, :], ACT.Exp, bias=neg_mx[:, e:e + 1],
                               accum_out=zsum[:, e:e + 1]).then_inc(exp_done, 1)

            def h_from_psum(bt, banks):
                for c in range(NC):
                    act.wait_ge(h_mm, NC * bt.n + c + 1)
                    if not isinstance(bt.n, int) or bt.n >= 2:
                        act.wait_ge(y_stored[c], 16 * (bt.n - 1))
                        act.wait_ge(stats_done, NC * (bt.n - 2) + c + 1)
                    elif bt.n == 1 and c == 0:
                        act.wait_ge(f1_stored, 16 * (B - 1))
                    act.copy(region[bt.par][:, cols(c)], banks[c][:, :]).then_inc(h_out, 1)

            def y_from_psum(bt):
                wait_l1(act, bt, NT - 1)
                for c in range(NC):
                    act.copy(region[bt.par][:, cols(c)], acc1[c][:, :]).then_inc(y_out, 1)

            def step(bt):
                nx = bt.next()
                for t in range(NT):
                    exp(bt, t)
                    if t + 2 < NT:
                        positive_part(bt, t + 2)
                    if is_first(bt) and 5 <= t < B + 4:
                        store_f1(t - 4)
                    if t == NT - 4 and not is_last(bt):
                        load_f1(nx)
                if not is_last(bt):
                    positive_part(nx, 0)
                if not is_first(bt):
                    y_from_psum(bt.prev())
                if not is_last(bt):
                    positive_part(nx, 1)
                    h_from_psum(nx, acc1)

            first = Batch(0, 0, 0)
            for c in range(NC):
                act.wait_ge(f1_mm, c + 1)
                act.copy(f1_all[0][:, cols(c)], acc0[c][:, :]).then_inc(f1_out, 1)
            act.wait_ge(f1_out, NC)
            positive_part(first, 0)
            positive_part(first, 1)
            h_from_psum(first, acc0)
            steps(act, step)
            y_from_psum(Batch(B - 1, (B - 1) // 2, 1))

            act.wait_ge(mv_done, 1)
            act.wait_ge(eps_set, 1)
            act.activation(bn[:, 0:1], mv[:, 1:2], ACT.Sqrt, bias=eps[:, 0:1]).then_inc(sqrt_done, 1)
            act.wait_ge(bn_done, 4)
            for b in [B - 1, *range(B - 1)]:
                if b == B - 1:
                    y = region[b % 2]
                else:
                    s = place["y", b]
                    act.wait_ge(slot_loaded[s], 16 * (earlier[s] + 1))
                    y = slots[s]
                act.activation(y[:, :], y[:, :], ACT.Relu, scale=bn[:, 2:3], bias=bn[:, 3:4]).then_inc(relu_done, 1)

        @block.vector
        def _(dve):
            def f_from_psum(b):
                dve.wait_ge(f_mm, b + 1)
                dve.tensor_copy(f12[:, b, :, :], acc1[0][:, 0:3 * NT]).then_inc(f_out, 1)

            def row_from_psum(b):
                dve.wait_ge(f_turned, b)
                if b > 1:
                    dve.wait_ge(f1_stored, 16 * (b - 1))
                dve.tensor_copy(f1_row[:, :], acc1[1][0:NT, 0:P]).then_inc(row_out, 1)

            def leaky(bt, t):
                e = t % ER
                dve.wait_ge(relu_out, NT * bt.n + t + 1)
                dve.scalar_tensor_tensor(out=scores[e][:, :], in0=scores[e][:, :], scalar=f12[:, bt.n, t, FA2:FA2 + 1],
                                         in1=f1_all[bt.par][:, :], op0=ALU.add, op1=ALU.add).then_inc(leaky_done, 1)

            def score(bt, t):
                e, s = t % ER, slot_of(bt.par, t)
                dve.wait_ge(leaky_done, NT * bt.n + t + 1)
                dve.wait_ge(slot_loaded[s], adj_value(bt, t))
                dve.sem_inc(score_begun, 1)
                dve.tensor_tensor_reduce(scores[e][:, :], scores[e][:, :], slots[s][:, :], 1.0, NEG_BIG,
                                         ALU.mult, ALU.max, mx[:, e:e + 1]).then_inc(max_done, 1)
                dve.wait_ge(max_done, NT * bt.n + t + 1)
                dve.tensor_scalar(neg_mx[:, e:e + 1], mx[:, e:e + 1], -1.0, None, ALU.mult).then_inc(neg_done, 1)

            def recip(bt, t):
                e = t % ER
                dve.wait_ge(exp_done, NT * bt.n + t + 1)
                wait_hz(bt, t)
                dve.reciprocal(rz[:, e:e + 1], zsum[:, e:e + 1]).then_inc(rz_done, 1)

            def wait_hz(bt, t):
                if not (is_first(bt) and t < ER):
                    dve.wait_ge(hz_done, NT * bt.n + t - ER + 1)

            def y_stats(bt):
                for c in range(NC):
                    dve.wait_ge(y_out, NC * bt.n + c + 1)
                    dve.bn_stats(stats[:, bt.n, c, :], region[bt.par][:, cols(c)]).then_inc(stats_done, 1)

            def make_xp(bt, c):
                dve.wait_ge(l0_chunk, NC * bt.n + c + 1)
                dve.wait_ge(xb_done, NC * bt.n + c + 1)
                dve.tensor_tensor(region[bt.par][:, cols(c)], acc0[c][:, :], region[bt.par][:, cols(c)],
                                  ALU.add).then_inc(xp_done, 1)

            def support_from_psum(bt, c):
                dve.wait_ge(sup_mm, NC * bt.n + c + 1)
                dve.wait_ge(xp_stored[c], 16 * (bt.n + 1))
                dve.tensor_tensor(region[bt.par][:, cols(c)].rearrange("p (t f) -> p t f", f=P),
                                  acc0[c][:, :].rearrange("p (t f) -> p t f", f=P),
                                  b1_sb[:, :].unsqueeze(1).to_broadcast([P, TC, P]), ALU.add).then_inc(sup_out, 1)

            def step(bt):
                nx = bt.next()
                for t in range(NT):
                    if t > 0 or is_first(bt):
                        leaky(bt, t)
                    if t > 1 or (t == 1 and is_first(bt)):
                        recip(bt, t - 1)
                    if t > 0 or is_first(bt):
                        score(bt, t)
                    if is_first(bt) and 2 <= t < B + 1:
                        f_from_psum(t - 1)
                    if is_first(bt) and 5 <= t < B + 4:
                        row_from_psum(t - 4)
                recip(bt, NT - 1)
                if not is_first(bt):
                    y_stats(bt.prev())
                for c in range(NC):
                    make_xp(bt, c)
                if not is_last(bt):
                    leaky(nx, 0)
                    score(nx, 0)
                for c in range(NC):
                    support_from_psum(bt, c)
                if not is_last(bt):
                    recip(nx, 0)

            dve.memset(eps[:, :], BN_EPS).then_inc(eps_set, 1)
            dve.wait_ge(wa_mm, 1)
            dve.tensor_scalar(wa_sb[:, FA1:FA2 + 1], acc1[2][:, 0:2], ALPHA, None, ALU.mult).then_inc(wa_out, 1)
            dve.tensor_scalar(wa_sb[:, FB2:FB2 + 1], acc1[2][:, 1:2], 1 - ALPHA, None, ALU.mult).then_inc(wa_out, 1)
            dve.wait_ge(wa_out, 1)
            dve.tensor_copy(wa1_cols, wa_sb[:, FA1:FA1 + 1].to_broadcast([P, P])).then_inc(wa_out, 1)
            f_from_psum(0)
            dve.wait_ge(b1_loaded, 16)
            steps(dve, step)
            y_stats(Batch(B - 1, (B - 1) // 2, 1))

            dve.wait_ge(stats_done, NC * B)
            dve.bn_aggr(mv[:, :], stats[:, :, :, :].rearrange("p b c s -> p (b c s)")).then_inc(mv_done, 1)
            dve.wait_ge(gb_loaded, 32)
            dve.wait_ge(sqrt_done, 1)
            dve.reciprocal(bn[:, 1:2], bn[:, 0:1]).then_inc(bn_done, 1)
            dve.wait_ge(bn_done, 1)
            dve.tensor_tensor(bn[:, 2:3], gb[:, 0:1], bn[:, 1:2], ALU.mult).then_inc(bn_done, 1)
            dve.wait_ge(bn_done, 2)
            dve.tensor_tensor(bn[:, 0:1], mv[:, 0:1], bn[:, 2:3], ALU.mult).then_inc(bn_done, 1)
            dve.wait_ge(bn_done, 3)
            dve.tensor_tensor(bn[:, 3:4], gb[:, 1:2], bn[:, 0:1], ALU.subtract).then_inc(bn_done, 1)
            for n, b in enumerate([B - 1, *range(B - 1)]):
                s = place["xp", b]
                y = region[b % 2] if b == B - 1 else slots[place["y", b]]
                dve.wait_ge(slot_loaded[s], 16 * (earlier[s] + 1))
                dve.wait_ge(relu_done, n + 1)
                dve.tensor_tensor(slots[s][:, :], slots[s][:, :], y[:, :], ALU.add).then_inc(sum_done, 1)

        @block.gpsimd
        def _(pool):
            def scale_h(bt, t):
                e = t % ER
                pool.wait_ge(rz_done, NT * bt.n + t + 1)
                if t % TC == 0:
                    pool.wait_ge(h_out, NC * bt.n + t // TC + 1)
                wait_ring(pool, bt, t)
                pool.tensor_tensor(hz[e][:, :], region[bt.par][:, tile_cols(t)],
                                   rz[:, e:e + 1].to_broadcast([P, P]), ALU.mult).then_inc(hz_done, 1)

            def add_bias(bt, c):
                if is_first(bt) and c == 0:
                    pool.wait_ge(bias_loaded, 16)
                pool.wait_ge(x_loaded[c], 16 * (bt.n + 1))
                pool.tensor_tensor(region[bt.par][:, cols(c)], region[bt.par][:, cols(c)],
                                   bias_sb[:, cols(c)], ALU.add).then_inc(xb_done, 1)

            def step(bt):
                for t in range(NT):
                    scale_h(bt, t)
                    if t == NT - 4 and not is_first(bt):
                        add_bias(bt, 0)
                for c in range(0 if is_first(bt) else 1, NC):
                    add_bias(bt, c)

            pool.memset(ident[:, :], 0.0).then_inc(ident_set, 1)
            pool.wait_ge(ident_set, 1)
            pool.affine_select(out=ident[:, :], in_=ident[:, :], compare_op=ALU.not_equal, fill=1.0,
                               base=0, pattern=[[-1, P]], channel_multiplier=1).then_inc(ident_set, 1)
            steps(pool, step)


NEG_BIG = -3.4028234663852886e38


def kernel(x, adj, L0_gnn_W, L0_gnn_a1, L0_gnn_a2, L0_gnn_bias, L1_gnn_W, L1_gnn_b, L1_gnn_gamma, L1_gnn_beta):
    import numpy as np
    import concourse.bacc as bacc
    from concourse.bass_utils import run_bass_kernel_spmd

    def lay(a):
        return np.ascontiguousarray(a)

    x, adj, W = np.asarray(x), np.asarray(adj), np.asarray(L0_gnn_W)
    arrays = {
        "adjT": lay(adj.transpose(0, 2, 1)),
        "xT": lay(x.transpose(0, 2, 1)),
        "biasT": lay(np.asarray(L0_gnn_bias).T),
        "W": lay(W),
        "WT": lay(W.T),
        "a12": lay(np.concatenate([np.asarray(L0_gnn_a1), np.asarray(L0_gnn_a2)], axis=1)),
        "W1": lay(L1_gnn_W),
        "b1": lay(L1_gnn_b),
        "gamma": lay(np.asarray(L1_gnn_gamma).reshape(-1, 1)),
        "beta": lay(np.asarray(L1_gnn_beta).reshape(-1, 1)),
    }
    nc = bacc.Bacc("TRN2", target_bir_lowering=False, num_devices=1, dynamic_dma_scratch_size=SCRATCH)
    args = [nc.dram_tensor(name, a.shape, F32, kind="ExternalInput").ap() for name, a in arrays.items()]
    out = nc.dram_tensor("outT", arrays["xT"].shape, F32, kind="ExternalOutput").ap()
    build(nc, *args, out)
    r = run_bass_kernel_spmd(nc, [arrays], core_ids=[0])
    return np.ascontiguousarray(np.asarray(r.results[0]["outT"]).transpose(0, 2, 1))
```

```python
from contextlib import ExitStack

import concourse.bass as bass
from concourse import mybir

F32 = mybir.dt.float32
F32R = mybir.dt.float32r
ALU = mybir.AluOpType
ACT = mybir.ActivationFunctionType

ALPHA = 0.2
BN_EPS = 1e-5
P = 128
FA1, FA2, FB2 = 2, 0, 1
SCRATCH = 1024


class Batch:

    def __init__(self, n, half, par):
        self.n, self.half, self.par = n, half, par

    def next(self):
        return Batch(self.n + 1, self.half if self.par == 0 else self.half + 1, 1 - self.par)

    def prev(self):
        return Batch(self.n - 1, self.half if self.par == 1 else self.half - 1, 1 - self.par)


def build(nc, adjT, xT, biasT, W, WT, a12, W1, b1, gamma, beta, outT):
    B, F, N = xT.shape
    NT = N // P
    CH = 512
    NC = N // CH
    TC = CH // P
    PRE = 2
    SLOTS = NT + PRE
    LEAD = 3
    ER = 4
    SPLIT = [1, 3, 4, 6, 7, 9, 10, 12, 13, 15]
    LAST_SPLIT = list(range(1, NT))
    WHOLE = [t for t in range(NT) if t not in SPLIT]
    NS = NC * len(SPLIT)
    SIGMA = list(range(PRE, NT - 2)) + [1, NT - 2, NT - 1, 0]
    assert NT % ER == 0 and len(SPLIT) % 2 == 0 and NT - 1 in SPLIT and 0 in WHOLE
    assert F == P and B == 8 and NT == 16 and sorted(SIGMA) == list(range(NT))

    def slot_of(par, t):
        return NT + t if (par and t < PRE) else t

    X_STAGE = {0: slot_of(1, 0), 1: slot_of(1, 1), **{b: NT - B + b for b in range(2, B)}}
    STAGED = set(X_STAGE[b] for b in range(1, B))
    F_STEP = {b: (3 * b - 2) // 2 for b in range(1, B)}
    ROWS_STEP, TURN_STEP = F_STEP[B - 1] + 1, NT - 2
    NF = 2 * (B - 1)

    with ExitStack() as ctx:
        def sb(name, shape, dt=F32):
            return ctx.enter_context(nc.sbuf_tensor(name, shape, dt))

        def sb_two_types(name, name_r, shape):
            place = -(-nc.sbuf_base // 32) * 32
            tensor = sb(name, shape)
            return tensor, nc.alloc_sbuf_tensor_at(name_r, shape, F32R, offset=place)

        def sem(name):
            return ctx.enter_context(nc.semaphore(name))

        f_rows = nc.dram_tensor("f_rows", [NF, N], F32, kind="Internal").ap()
        xp_dram = nc.dram_tensor("xp_dram", [B, P, N], F32, kind="Internal").ap()
        y_dram = nc.dram_tensor("y_dram", [B, P, N], F32, kind="Internal").ap()

        slots, slots_lo = zip(*[sb_two_types(f"adj_slot{s}", f"adj_lo{s}", [P, N]) for s in range(SLOTS)])
        scores, exp_lo = zip(*[sb_two_types(f"scores{e}", f"exp_lo{e}", [P, N]) for e in range(ER)])
        f1_odd, sup_lo = sb_two_types("f1_odd", "sup_lo", [P, N])
        f1_all = [sb("f1_even", [P, N]), f1_odd]
        region = [sb("region_even", [P, N]), sb("region_odd", [P, N])]
        exp_hi = [sb(f"exp_hi{c}", [P, CH], F32R) for c in range(NC)]
        hz, hz_lo = zip(*[sb_two_types(f"hz{e}", f"hz_lo{e}", [P, P]) for e in range(ER)])
        hz_hi = [sb(f"hz_hi{e}", [P, P], F32R) for e in range(2)]
        w_sb = sb("w_sb", [P, P])
        w1_sb = sb("w1_sb", [P, P])
        b1_sb = sb("b1_sb", [P, P])
        a12_sb = sb("a12_sb", [P, 2])
        wa_sb = sb("wa_sb", [P, 3])
        f12 = sb("f12", [P, B, NT, 2])
        mx = sb("mx", [P, ER])
        neg_mx = sb("neg_mx", [P, ER])
        zsum = sb("zsum", [P, ER])
        rz = sb("rz", [P, ER])
        stats = sb("stats", [P, B, NC, 6])
        mv = sb("mv", [P, 2])
        gb = sb("gb", [P, 2])
        eps = sb("eps", [P, 1])
        bn = sb("bn", [P, 4])
        wt_sb = scores[ER - 1][:, 0:P]
        ident = region[1][:, 0:P]
        f2_grid = region[1][0:(B - 1) * NT, P:2 * P]
        wa1_cols = region[1][:, 2 * P:3 * P]
        wa_rows = region[1][:, 3 * P:3 * P + (B - 1) * (NF + 1)]
        f_sb = f1_all[1][0:NF, :]
        acc0 = [ctx.enter_context(nc.psum_tensor(f"acc0_{c}", [P, CH], F32)) for c in range(NC)]
        acc1 = [ctx.enter_context(nc.psum_tensor(f"acc1_{c}", [P, CH], F32)) for c in range(NC)]

        slot_loaded = [sem(f"slot_loaded{s}") for s in range(SLOTS)]
        wt_loaded, w_loaded, w1_loaded = sem("wt_loaded"), sem("w_loaded"), sem("w1_loaded")
        a12_loaded, b1_loaded = sem("a12_loaded"), sem("b1_loaded")
        bias_loaded = [sem(f"bias_loaded{c}") for c in range(NC)]
        gb_loaded = sem("gb_loaded")
        f2_loaded = sem("f2_loaded")
        f_stored, f1_loaded = sem("f_stored"), [sem("f1_loaded_even"), sem("f1_loaded_odd")]
        x0_loaded = [sem(f"x0_loaded{c}") for c in range(NC)]
        x_loaded = [sem(f"x_loaded{c}") for c in range(NC)]
        xp_stored = [sem(f"xp_stored{c}") for c in range(NC)]
        y_stored = [sem(f"y_stored{c}") for c in range(NC)]
        out_stored = sem("out_stored")
        wa_mm, f1_mm, f_mm, f_turned = sem("wa_mm"), sem("f1_mm"), sem("f_mm"), sem("f_turned")
        h_mm, sup_mm = sem("h_mm"), sem("sup_mm")
        whole_used = sem("whole_used")
        split_used = sem("split_used")
        l1_tile, l1_chunk = sem("l1_tile"), sem("l1_chunk")
        f1_out, row_out = sem("f1_out"), sem("row_out")
        hi_done, lo_done = sem("hi_done"), sem("lo_done")
        sup_hi_done, sup_lo_done = sem("sup_hi_done"), sem("sup_lo_done")
        adj_hi_done, adj_lo_done = sem("adj_hi_done"), sem("adj_lo_done")
        relu_out, neg_done, exp_done = sem("relu_out"), sem("neg_done"), sem("exp_done")
        h_out, y_out, sqrt_done, relu_done = sem("h_out"), sem("y_out"), sem("sqrt_done"), sem("relu_done")
        wa_out, f_out = sem("wa_out"), sem("f_out")
        leaky_done, score_begun = sem("leaky_done"), sem("score_begun")
        max_done, rz_done = sem("max_done"), sem("rz_done")
        xp_done, sup_out, stats_done = sem("xp_done"), sem("sup_out"), sem("stats_done")
        eps_set, mv_done, bn_done, sum_done = sem("eps_set"), sem("mv_done"), sem("bn_done"), sem("sum_done")
        hz_scaled = sem("hz_scaled")
        ident_set, hz_done, xb_done = sem("ident_set"), sem("hz_done"), sem("xb_done")

        def cols(c):
            return slice(c * CH, (c + 1) * CH)

        def tile_cols(t):
            return slice(t * P, (t + 1) * P)

        def adj_value(bt, t):
            if t == 0:
                return 16 * (bt.half + 1)
            if t < PRE:
                return 16 * (bt.n + 1)
            return 16 * (bt.n + 1 + (t in STAGED))

        def chunk_count(bt, t, c):
            return NS * bt.n + NC * SPLIT.index(t) + c + 1

        def wait_l0(eng, bt, t):
            if t in SPLIT:
                eng.wait_ge(split_used, chunk_count(bt, t, NC - 1))
            else:
                eng.wait_ge(whole_used, len(WHOLE) * bt.n + WHOLE.index(t) + 1)

        def wait_l1(eng, bt, k):
            if k == NT - 1:
                eng.wait_ge(l1_chunk, NC * (bt.n + 1))
            else:
                eng.wait_ge(l1_tile, (NT - 1) * bt.n + k + 1)

        def wait_ring(eng, bt, t):
            if t >= ER:
                wait_l0(eng, bt, t - ER)
            elif not is_first(bt):
                wait_l0(eng, bt.prev(), t - ER + NT)

        def is_first(bt):
            return isinstance(bt.n, int) and bt.n == 0

        def is_last(bt):
            return isinstance(bt.n, int) and bt.n == B - 1

        def steps(eng, step):
            step(Batch(0, 0, 0))
            with eng.Fori(0, (B - 2) // 2) as i:
                step(Batch(2 * i + 1, i, 1))
                step(Batch(2 * i + 2, i + 1, 0))
            step(Batch(B - 1, (B - 1) // 2, 1))

        loads = [(y_dram, b, "y") for b in range(B - 1)]
        order = [("xp", B - 1)] + [x for b in range(B - 1) for x in (("y", b), ("xp", b))]
        places = list(range(PRE)) + [slot_of(1, t) for t in SIGMA]
        home = dict(zip(order, places))
        earlier = {s: 0 for s in range(SLOTS)}
        for b in range(B):
            for t in range(NT):
                earlier[slot_of(b % 2, t)] += 1
        for s in STAGED:
            earlier[s] += 1
        for b in range(2, B):
            earlier[slot_of(b % 2, 1)] += 1

        pieces = [(b, cols(c)) for b in (B - 1, 0) for c in range(NC)] + [(b, slice(0, N)) for b in range(1, B - 1)]

        block = ctx.enter_context(nc.Block())

        @block.sync
        def _(sp):
            def load_adj(bt, t):
                s = slot_of(bt.par, t)
                sp.dma_start(slots[s][:, :], adjT[bt.n, tile_cols(t), :]).then_inc(slot_loaded[s], 16)

            def load_x(b, s):
                sp.dma_start(slots[s][:, :], xT[b]).then_inc(slot_loaded[s], 16)

            def load_residual(bt, c):
                sp.wait_ge(hz_done, NT * bt.n + TC * (c + 1))
                sp.dma_start(region[bt.par][:, cols(c)], xT[bt.n][:, cols(c)]).then_inc(x_loaded[c], 16)

            def load_f1(bt):
                if not (isinstance(bt.n, int) and bt.n < 2):
                    sp.wait_ge(xb_done, NC * (bt.n - 1))
                sp.dma_start(f1_all[bt.par][:, :], f_rows[bt.n - 1].partition_broadcast(P)).then_inc(f1_loaded[bt.par], 16)

            def load_bias(bt):
                sp.wait_ge(leaky_done, NT * (bt.n + 1))
                for c in range(NC):
                    sp.dma_start(f1_all[bt.par][:, cols(c)], biasT[:, cols(c)]).then_inc(bias_loaded[c], 16)

            def store_xp(bt):
                for c in range(NC):
                    sp.wait_ge(xp_done, NC * bt.n + c + 1)
                    sp.dma_start(xp_dram[bt.n][:, cols(c)], region[bt.par][:, cols(c)]).then_inc(xp_stored[c], 16)

            def step(bt):
                nx = bt.next()
                if is_first(bt):
                    for t in range(1, NT):
                        for b in F_STEP:
                            if max(F_STEP[b], 1) == t:
                                load_x(b, X_STAGE[b])
                        if t in STAGED:
                            sp.wait_ge(f_mm, t - (NT - B) + 2)
                        load_adj(bt, t)
                    sp.wait_ge(row_out, NC)
                    sp.dma_start(f_rows, f_sb).then_inc(f_stored, 16)
                    sp.wait_ge(f_stored, 16)
                    sp.dma_start(f2_grid, f_rows[B - 1:NF].rearrange("b (t p) -> (b t) p", p=P)).then_inc(f2_loaded, 16)
                    load_f1(nx)
                    sp.wait_ge(h_mm, NC)
                    load_adj(nx, 0)
                    for c in range(NC - 1):
                        load_residual(bt, c)
                    load_bias(bt)
                    load_residual(bt, NC - 1)
                else:
                    pv = bt.prev()
                    for k, t in enumerate(SIGMA):
                        wait_l1(sp, pv, k)
                        if t >= PRE:
                            load_adj(bt, t)
                        elif not is_last(bt):
                            if t == 1:
                                load_x(nx.n, slot_of(nx.par, 1))
                            else:
                                load_adj(nx, 0)
                        if k == 11 and not is_last(bt):
                            load_f1(nx)
                        if k == 7:
                            load_residual(bt, 0)
                        if k == 11:
                            load_residual(bt, 1)
                        if k == 14:
                            load_residual(bt, 2)
                        if k == 14:
                            load_bias(bt)
                    load_residual(bt, 3)
                    for c in range(NC):
                        sp.wait_ge(y_out, NC * pv.n + c + 1)
                        sp.dma_start(y_dram[pv.n][:, cols(c)], region[pv.par][:, cols(c)]).then_inc(y_stored[c], 16)
                store_xp(bt)
                if not is_last(bt):
                    sp.wait_ge(h_mm, NC * (nx.n + 1))
                    load_adj(nx, 1)

            sp.dma_start(wt_sb[:, :], WT).then_inc(wt_loaded, 16)
            sp.dma_start(a12_sb[:, :], a12).then_inc(a12_loaded, 16)
            for c in range(NC):
                sp.dma_start(slots[X_STAGE[0]][:, cols(c)], xT[0][:, cols(c)]).then_inc(x0_loaded[c], 16)
            sp.dma_start(w_sb[:, :], W).then_inc(w_loaded, 16)
            load_adj(Batch(0, 0, 0), 0)
            sp.dma_start(w1_sb[:, :], W1).then_inc(w1_loaded, 16)
            sp.dma_start(b1_sb[:, :], b1.partition_broadcast(P)).then_inc(b1_loaded, 16)
            sp.dma_start(gb[:, 0:1], gamma).then_inc(gb_loaded, 16)
            sp.dma_start(gb[:, 1:2], beta).then_inc(gb_loaded, 16)
            steps(sp, step)

            for c in range(NC):
                sp.wait_ge(y_stored[c], 16 * (B - 1))
                sp.wait_ge(xp_stored[c], 16 * B)
            for n, (what, b) in enumerate(order):
                if n >= PRE:
                    wait_l1(sp, Batch(B - 1, (B - 1) // 2, 1), n - PRE)
                s = home[what, b]
                src = y_dram if what == "y" else xp_dram
                sp.dma_start(slots[s][:, :], src[b]).then_inc(slot_loaded[s], 16)
            for n, (b, piece) in enumerate(pieces):
                sp.wait_ge(sum_done, n + 1)
                sp.dma_start(outT[b][:, piece], slots[home["xp", b]][:, piece]).then_inc(out_stored, 16)
            sp.wait_ge(out_stored, 16 * len(pieces))

        @block.tensor
        def _(pe):
            def f_columns(tiles, bank):
                for t in tiles:
                    mm = pe.matmul(bank[:, 3 * t:3 * t + 3], slots[X_STAGE[0]][:, tile_cols(t)], wa_sb[:, :],
                                   start=True, stop=True)
                mm.then_inc(f_mm, 1)

            def rows_of_f(b):
                pe.wait_ge(slot_loaded[X_STAGE[b]], 16)
                if b == 1:
                    pe.wait_ge(f_out, 2)
                    pe.wait_ge(wa_out, 7)
                for c in range(NC):
                    mm = pe.matmul(acc1[c][0:NF, :], wa_rows[:, (b - 1) * NF:b * NF], slots[X_STAGE[b]][:, cols(c)],
                                   start=(b == 1), stop=(b == B - 1))
                mm.then_inc(f_mm, 1)

            def turn_f2():
                pe.wait_ge(row_out, NC)
                pe.wait_ge(ident_set, 2)
                pe.wait_ge(f2_loaded, 16)
                pe.transpose(acc1[0][:, 0:(B - 1) * NT], f2_grid, ident[0:(B - 1) * NT, 0:(B - 1) * NT])\
                    .then_inc(f_turned, 1)

            def make_h(bt, x, banks, c):
                if not isinstance(bt.n, int) or bt.n >= 2:
                    pe.wait_ge(y_out, NC * (bt.n - 2) + c + 1)
                for q in range(TC):
                    mm = pe.matmul(banks[c][:, tile_cols(q)], x[:, tile_cols(TC * c + q)], w_sb[:, :],
                                   start=True, stop=True)
                mm.then_inc(h_mm, 1)

            def wait_acc0(bt, t, c):
                if t == 0 and is_first(bt):
                    pe.wait_ge(h_out, c + 1)
                elif t == 0:
                    pe.wait_ge(sup_out, NC * (bt.n - 1) + c + 1)

            def layer0(bt, t):
                e = t % ER
                pe.wait_ge(exp_done, NT * bt.n + t + 1)
                pe.wait_ge(hz_done, NT * bt.n + t + 1)
                for c in range(NC):
                    wait_acc0(bt, t, c)
                    mm = pe.matmul(acc0[c][:, :], hz[e][:, :], scores[e][:, cols(c)],
                                   start=(t == 0), stop=(t == NT - 1))
                    if t in SPLIT:
                        mm.then_inc(split_used, 1)
                if t in WHOLE:
                    mm.then_inc(whole_used, 1)

            def layer0_split(bt, t):
                e, m = t % ER, SPLIT.index(t)
                pe.wait_ge(hz_done, NT * bt.n + t + 1)
                for c in range(NC):
                    pe.wait_ge(lo_done, chunk_count(bt.prev(), t, c))
                    pe.matmul(acc0[c][:, :], hz_lo[e][:, :], exp_hi[c][:, :], start=False, stop=False)
                    pe.matmul(acc0[c][:, :], hz_hi[m % 2][:, :], exp_hi[c][:, :], start=False, stop=False)
                    pe.matmul(acc0[c][:, :], hz_hi[m % 2][:, :], exp_lo[e][:, cols(c)], start=False,
                              stop=(t == NT - 1)).then_inc(split_used, 1)

            def make_support(bt, c):
                pe.wait_ge(xp_done, NC * bt.n + c + 1)
                for q in range(TC):
                    mm = pe.matmul(acc0[c][:, tile_cols(q)], region[bt.par][:, tile_cols(TC * c + q)], w1_sb[:, :],
                                   start=True, stop=True)
                mm.then_inc(sup_mm, 1)

            def layer1(bt, k, last=False):
                t = SIGMA[k]
                if k == 0 or t % TC == 0:
                    pe.wait_ge(sup_out, NC * bt.n + t // TC + 1)
                for c in range(NC):
                    if k == 0 and not last:
                        pe.wait_ge(h_out, NC * (bt.n + 1) + c + 1)
                    elif k == 0:
                        pe.wait_ge(y_out, NC * (bt.n - 1) + c + 1)
                    mm = pe.matmul(acc1[c][:, :], region[bt.par][:, tile_cols(t)],
                                   slots[slot_of(bt.par, t)][:, cols(c)], start=(k == 0), stop=(k == NT - 1))
                    if k == NT - 1:
                        mm.then_inc(l1_chunk, 1)
                if k < NT - 1:
                    mm.then_inc(l1_tile, 1)

            def layer1_split(bt, k):
                t, m = SIGMA[k], LAST_SPLIT.index(k)
                pe.wait_ge(sup_lo_done, t // TC + 1)
                pe.wait_ge(adj_lo_done, m + 1)
                sup_hi = exp_hi[t // TC][:, tile_cols(t % TC)]
                for c in range(NC):
                    pe.matmul(acc1[c][:, :], sup_lo[:, tile_cols(t)], exp_lo[m % ER][:, cols(c)],
                              start=False, stop=False)
                    pe.matmul(acc1[c][:, :], sup_hi, exp_lo[m % ER][:, cols(c)], start=False, stop=False)
                    mm = pe.matmul(acc1[c][:, :], sup_hi, slots_lo[slot_of(bt.par, t)][:, cols(c)],
                                   start=False, stop=(k == NT - 1))
                    if k == NT - 1:
                        mm.then_inc(l1_chunk, 1)
                if k < NT - 1:
                    mm.then_inc(l1_tile, 1)

            def step(bt):
                nx = bt.next()
                ahead = 0
                for t in range(NT):
                    if is_first(bt):
                        for b in F_STEP:
                            if F_STEP[b] == t:
                                rows_of_f(b)
                        if t == TURN_STEP:
                            turn_f2()
                    else:
                        while ahead < min(t + (LEAD if t > 0 else LEAD - 1), NT):
                            layer1(bt.prev(), ahead)
                            ahead += 1
                    if t in SPLIT and not is_first(bt):
                        layer0_split(bt, t)
                    else:
                        layer0(bt, t)
                if is_first(bt):
                    pe.wait_ge(f_out, 4)
                    pe.wait_ge(slot_loaded[X_STAGE[1]], 16)
                elif not is_last(bt):
                    pe.wait_ge(slot_loaded[slot_of(nx.par, 1)], 16 * nx.n)
                for c in range(NC):
                    if not is_last(bt):
                        make_h(nx, slots[slot_of(nx.par, 1)], acc1, c)
                    make_support(bt, c)

            pe.wait_ge(wt_loaded, 16)
            pe.wait_ge(a12_loaded, 16)
            pe.matmul(acc1[2][:, 0:2], wt_sb, a12_sb[:, :], start=True, stop=True).then_inc(wa_mm, 1)
            pe.wait_ge(wa_out, 4)
            for c in range(NC):
                pe.wait_ge(x0_loaded[c], 16)
                if c == 0:
                    f_columns([0], acc1[3])
                pe.matmul(acc0[c][:, :], wa1_cols, slots[X_STAGE[0]][:, cols(c)], start=True, stop=True)\
                    .then_inc(f1_mm, 1)
            f_columns(range(1, NT), acc1[0])
            pe.wait_ge(w_loaded, 16)
            for c in range(NC):
                pe.wait_ge(f1_out, c + 1)
                make_h(Batch(0, 0, 0), slots[X_STAGE[0]], acc0, c)
            pe.wait_ge(w1_loaded, 16)
            steps(pe, step)
            last = Batch(B - 1, (B - 1) // 2, 1)
            for k in range(NT):
                if k in LAST_SPLIT:
                    layer1_split(last, k)
                else:
                    layer1(last, k, last=True)

        @block.scalar
        def _(act):
            def positive_part(bt, t):
                if t == 0 and not is_first(bt):
                    act.wait_ge(f1_loaded[bt.par], 16 * (bt.half + bt.par))
                if t == 0 and is_first(bt):
                    act.wait_ge(f_out, 1)
                if t == 0 and isinstance(bt.n, int) and bt.n == 1:
                    act.wait_ge(f_out, 4)
                if t == 1 and is_first(bt):
                    act.wait_ge(f_out, 2)
                wait_ring(act, bt, t)
                act.activation(scores[t % ER][:, :], f1_all[bt.par][:, :], ACT.Relu, scale=(1 - ALPHA) / ALPHA,
                               bias=f12[:, bt.n, t, FB2:FB2 + 1]).then_inc(relu_out, 1)

            def exp(bt, t):
                e = t % ER
                act.wait_ge(max_done, NT * bt.n + t + 1)
                act.mul(neg_mx[:, e:e + 1], mx[:, e:e + 1], -1.0).then_inc(neg_done, 1)
                act.wait_ge(neg_done, NT * bt.n + t + 1)
                act.activation(scores[e][:, :], scores[e][:, :], ACT.Exp, bias=neg_mx[:, e:e + 1],
                               accum_out=zsum[:, e:e + 1]).then_inc(exp_done, 1)

            def exp_high(bt, t):
                e, m = t % ER, SPLIT.index(t)
                act.wait_ge(exp_done, NT * bt.n + t + 1)
                for c in range(NC):
                    act.wait_ge(split_used, NS * bt.n + NC * (m - 1) + c + 1)
                    act.copy(exp_hi[c][:, :], scores[e][:, cols(c)]).then_inc(hi_done, 1)

            def adj_high(bt, m):
                t = SIGMA[LAST_SPLIT[m]]
                act.wait_ge(slot_loaded[slot_of(bt.par, t)], adj_value(bt, t))
                if m < ER:
                    wait_l0(act, bt, NT - ER + m)
                else:
                    wait_l1(act, bt, LAST_SPLIT[m - ER])
                act.copy(exp_lo[m % ER][:, :], slots[slot_of(bt.par, t)][:, :]).then_inc(adj_hi_done, 1)

            def support_high(bt):
                for c in range(NC):
                    act.wait_ge(sup_out, NC * bt.n + c + 1)
                    act.copy(exp_hi[c][:, :], region[bt.par][:, cols(c)]).then_inc(sup_hi_done, 1)

            def h_from_psum(bt, banks, chunks=range(NC)):
                for c in chunks:
                    act.wait_ge(h_mm, NC * bt.n + c + 1)
                    if not isinstance(bt.n, int) or bt.n >= 2:
                        act.wait_ge(y_stored[c], 16 * (bt.n - 1))
                        act.wait_ge(stats_done, NC * (bt.n - 2) + c + 1)
                    elif bt.n == 1 and c == 0:
                        act.wait_ge(f_turned, 1)
                    act.copy(region[bt.par][:, cols(c)], banks[c][:, :]).then_inc(h_out, 1)

            def y_from_psum(bt):
                wait_l1(act, bt, NT - 1)
                for c in range(NC):
                    act.copy(region[bt.par][:, cols(c)], acc1[c][:, :]).then_inc(y_out, 1)

            def step(bt):
                nx = bt.next()
                for t in range(NT):
                    exp(bt, t)
                    if t == 0 and is_first(bt):
                        h_from_psum(bt, acc0, [2, 3])
                    if t + 2 < NT:
                        positive_part(bt, t + 2)
                    if is_first(bt) and t == ROWS_STEP:
                        act.wait_ge(f_mm, B + 1)
                        for c in range(NC):
                            act.copy(f_sb[:, cols(c)], acc1[c][0:NF, :]).then_inc(row_out, 1)
                    if t + (1 if is_first(bt) else 2) == NT and not is_last(bt):
                        positive_part(nx, 0)
                    if t in SPLIT and not is_first(bt):
                        exp_high(bt, t)
                if not is_first(bt):
                    y_from_psum(bt.prev())
                if not is_last(bt):
                    positive_part(nx, 1)
                    h_from_psum(nx, acc1)

            first = Batch(0, 0, 0)
            for c in range(NC):
                act.wait_ge(f1_mm, c + 1)
                act.copy(f1_all[0][:, cols(c)], acc0[c][:, :]).then_inc(f1_out, 1)
            act.wait_ge(f1_out, NC)
            positive_part(first, 0)
            positive_part(first, 1)
            h_from_psum(first, acc0, [0, 1])
            steps(act, step)
            last = Batch(B - 1, (B - 1) // 2, 1)
            adj_high(last, 0)
            adj_high(last, 1)
            support_high(last)
            for m in range(2, len(LAST_SPLIT)):
                adj_high(last, m)
            act.wait_ge(eps_set, 1)
            act.activation(bn[:, 1:2], eps[:, 0:1], ACT.Sqrt).then_inc(sqrt_done, 1)

            act.wait_ge(mv_done, 1)
            act.activation(bn[:, 0:1], mv[:, 1:2], ACT.Sqrt, bias=eps[:, 0:1]).then_inc(sqrt_done, 1)
            act.wait_ge(bn_done, 4)
            for n, (b, piece) in enumerate(pieces):
                if b == B - 1:
                    act.wait_ge(y_stored[n], 16 * (B - 1))
                    y, normed = acc1[n][:, :], region[0][:, piece]
                else:
                    s = home["y", b]
                    act.wait_ge(slot_loaded[s], 16 * (earlier[s] + 1))
                    y = normed = slots[s][:, piece]
                act.activation(normed, y, ACT.Relu, scale=bn[:, 2:3], bias=bn[:, 3:4]).then_inc(relu_done, 1)

        @block.vector
        def _(dve):
            def f_from_psum():
                dve.wait_ge(f_turned, 1)
                f2 = acc1[0][:, 0:(B - 1) * NT].rearrange("p (b t) -> p b t", t=NT)
                dve.tensor_copy(f12[:, 1:B, :, FA2], f2).then_inc(f_out, 1)
                dve.tensor_scalar(f12[:, 1:B, :, FB2], f2, (1 - ALPHA) / ALPHA, None, ALU.mult).then_inc(f_out, 1)

            def leaky(bt, t):
                e = t % ER
                dve.wait_ge(relu_out, NT * bt.n + t + 1)
                dve.scalar_tensor_tensor(out=scores[e][:, :], in0=scores[e][:, :], scalar=f12[:, bt.n, t, FA2:FA2 + 1],
                                         in1=f1_all[bt.par][:, :], op0=ALU.add, op1=ALU.add).then_inc(leaky_done, 1)

            def score(bt, t):
                e, s = t % ER, slot_of(bt.par, t)
                dve.wait_ge(leaky_done, NT * bt.n + t + 1)
                dve.wait_ge(slot_loaded[s], adj_value(bt, t))
                dve.sem_inc(score_begun, 1)
                dve.tensor_tensor_reduce(scores[e][:, :], scores[e][:, :], slots[s][:, :], 1.0, NEG_BIG,
                                         ALU.mult, ALU.max, mx[:, e:e + 1]).then_inc(max_done, 1)

            def recip(bt, t):
                e = t % ER
                dve.wait_ge(exp_done, NT * bt.n + t + 1)
                wait_hz(bt, t)
                dve.reciprocal(rz[:, e:e + 1], zsum[:, e:e + 1]).then_inc(rz_done, 1)

            def wait_hz(bt, t):
                if not (is_first(bt) and t < ER):
                    dve.wait_ge(hz_done, NT * bt.n + t - ER + 1)

            def exp_low(bt, t):
                e, m = t % ER, SPLIT.index(t)
                for c in range(NC):
                    dve.wait_ge(hi_done, chunk_count(bt.prev(), t, c))
                    dve.tensor_tensor(exp_lo[e][:, cols(c)], scores[e][:, cols(c)], exp_hi[c][:, :].bitcast(F32),
                                      ALU.subtract).then_inc(lo_done, 1)

            def adj_low(bt, m):
                t = SIGMA[LAST_SPLIT[m]]
                s = slot_of(bt.par, t)
                dve.wait_ge(adj_hi_done, m + 1)
                dve.tensor_tensor(slots_lo[s][:, :], slots[s][:, :], exp_lo[m % ER][:, :].bitcast(F32),
                                  ALU.subtract).then_inc(adj_lo_done, 1)

            def support_low(bt):
                for c in range(NC):
                    dve.wait_ge(sup_hi_done, c + 1)
                    dve.tensor_tensor(sup_lo[:, cols(c)], region[bt.par][:, cols(c)], exp_hi[c][:, :].bitcast(F32),
                                      ALU.subtract).then_inc(sup_lo_done, 1)

            def y_stats(bt):
                for c in range(NC):
                    dve.wait_ge(y_out, NC * bt.n + c + 1)
                    dve.bn_stats(stats[:, bt.n, c, :], region[bt.par][:, cols(c)]).then_inc(stats_done, 1)

            def make_xp(bt, c):
                dve.wait_ge(split_used, chunk_count(bt, NT - 1, c))
                dve.wait_ge(xb_done, NC * bt.n + c + 1)
                dve.tensor_tensor(region[bt.par][:, cols(c)], acc0[c][:, :], region[bt.par][:, cols(c)],
                                  ALU.add).then_inc(xp_done, 1)

            def support_from_psum(bt, c):
                dve.wait_ge(sup_mm, NC * bt.n + c + 1)
                dve.wait_ge(xp_stored[c], 16 * (bt.n + 1))
                dve.tensor_tensor(region[bt.par][:, cols(c)].rearrange("p (t f) -> p t f", f=P),
                                  acc0[c][:, :].rearrange("p (t f) -> p t f", f=P),
                                  b1_sb[:, :].unsqueeze(1).to_broadcast([P, TC, P]), ALU.add).then_inc(sup_out, 1)

            def step(bt):
                nx = bt.next()
                for t in range(NT):
                    if t > 0 or is_first(bt):
                        score(bt, t)
                    if t + 1 < NT:
                        leaky(bt, t + 1)
                    elif not is_first(bt) and not is_last(bt):
                        leaky(nx, 0)
                    if t - 1 in SPLIT and not is_first(bt):
                        exp_low(bt, t - 1)
                    if t > 0 or is_first(bt):
                        recip(bt, t)
                    if is_first(bt) and t == TURN_STEP + 1:
                        f_from_psum()
                if is_first(bt):
                    leaky(nx, 0)
                else:
                    exp_low(bt, NT - 1)
                if not is_first(bt):
                    y_stats(bt.prev())
                for c in range(NC):
                    make_xp(bt, c)
                if not is_last(bt):
                    score(nx, 0)
                else:
                    adj_low(bt, 0)
                for c in range(NC):
                    support_from_psum(bt, c)
                if not is_last(bt):
                    recip(nx, 0)

            dve.memset(eps[:, :], BN_EPS).then_inc(eps_set, 1)
            dve.wait_ge(wa_mm, 1)
            dve.tensor_scalar(wa_sb[:, FA1:FA1 + 1], acc1[2][:, 0:1], ALPHA, None, ALU.mult).then_inc(wa_out, 1)
            dve.tensor_scalar(wa_sb[:, FA2:FA2 + 1], acc1[2][:, 1:2], ALPHA, None, ALU.mult).then_inc(wa_out, 1)
            dve.tensor_scalar(wa_sb[:, FB2:FB2 + 1], acc1[2][:, 1:2], 1 - ALPHA, None, ALU.mult).then_inc(wa_out, 1)
            dve.wait_ge(wa_out, 3)
            dve.tensor_copy(wa1_cols, wa_sb[:, FA1:FA1 + 1].to_broadcast([P, P])).then_inc(wa_out, 1)
            dve.wait_ge(f_mm, 1)
            dve.tensor_copy(f12[:, 0, 0, :], acc1[3][:, 0:2]).then_inc(f_out, 1)
            leaky(Batch(0, 0, 0), 0)
            dve.wait_ge(f_mm, 2)
            dve.tensor_copy(f12[:, 0, 1:NT, :],
                            acc1[0][:, 0:3 * NT].rearrange("p (t k) -> p t k", k=3)[:, 1:NT, 0:2]).then_inc(f_out, 1)
            dve.memset(wa_rows, 0.0).then_inc(wa_out, 1)
            dve.wait_ge(wa_out, 5)
            own = wa_rows.rearrange("p (b k) -> p b k", k=NF + 1)
            dve.tensor_copy(own[:, :, 0], wa_sb[:, FA1:FA1 + 1].to_broadcast([P, B - 1])).then_inc(wa_out, 1)
            dve.tensor_copy(own[:, :, B - 1], wa_sb[:, FA2:FA2 + 1].to_broadcast([P, B - 1])).then_inc(wa_out, 1)
            dve.wait_ge(b1_loaded, 16)
            steps(dve, step)
            support_low(Batch(B - 1, (B - 1) // 2, 1))
            for m in range(1, len(LAST_SPLIT)):
                adj_low(Batch(B - 1, (B - 1) // 2, 1), m)
            for c in range(NC):
                dve.wait_ge(l1_chunk, NC * (B - 1) + c + 1)
                dve.bn_stats(stats[:, B - 1, c, :], acc1[c][:, :]).then_inc(stats_done, 1)

            dve.wait_ge(stats_done, NC * B)
            dve.bn_aggr(mv[:, :], stats[:, :, :, :].rearrange("p b c s -> p (b c s)")).then_inc(mv_done, 1)
            dve.wait_ge(gb_loaded, 32)
            dve.wait_ge(sqrt_done, 2)
            dve.reciprocal(bn[:, 1:2], bn[:, 0:1]).then_inc(bn_done, 1)
            dve.wait_ge(bn_done, 1)
            dve.tensor_tensor(bn[:, 2:3], gb[:, 0:1], bn[:, 1:2], ALU.mult).then_inc(bn_done, 1)
            dve.wait_ge(bn_done, 2)
            dve.tensor_tensor(bn[:, 0:1], mv[:, 0:1], bn[:, 2:3], ALU.mult).then_inc(bn_done, 1)
            dve.wait_ge(bn_done, 3)
            dve.tensor_tensor(bn[:, 3:4], gb[:, 1:2], bn[:, 0:1], ALU.subtract).then_inc(bn_done, 1)
            for n, (b, piece) in enumerate(pieces):
                s = home["xp", b]
                normed = region[0] if b == B - 1 else slots[home["y", b]]
                dve.wait_ge(slot_loaded[s], 16 * (earlier[s] + 1))
                dve.wait_ge(relu_done, n + 1)
                dve.tensor_tensor(slots[s][:, piece], slots[s][:, piece], normed[:, piece], ALU.add)\
                    .then_inc(sum_done, 1)

        @block.gpsimd
        def _(pool):
            def scale_h(bt, t):
                e = t % ER
                pool.wait_ge(rz_done, NT * bt.n + t + 1)
                if t % TC == 0:
                    pool.wait_ge(h_out, NC * bt.n + t // TC + 1)
                wait_ring(pool, bt, t)
                scaled = pool.tensor_tensor(hz[e][:, :], region[bt.par][:, tile_cols(t)],
                                            rz[:, e:e + 1].to_broadcast([P, P]), ALU.mult)
                if t in WHOLE or is_first(bt):
                    scaled.then_inc(hz_done, 1)
                    return
                scaled.then_inc(hz_scaled, 1)
                m = SPLIT.index(t)
                pool.wait_ge(split_used, NS * bt.n + NC * (m - 1))
                pool.tensor_tensor(hz_hi[m % 2][:, :], region[bt.par][:, tile_cols(t)],
                                   rz[:, e:e + 1].to_broadcast([P, P]), ALU.mult).then_inc(hz_scaled, 1)
                pool.wait_ge(hz_scaled, 2 * (len(SPLIT) * (bt.n - 1) + m + 1))
                pool.tensor_tensor(hz_lo[e][:, :], hz[e][:, :], hz_hi[m % 2][:, :].bitcast(F32),
                                   ALU.subtract).then_inc(hz_done, 1)

            def add_bias(bt, c):
                pool.wait_ge(x_loaded[c], 16 * (bt.n + 1))
                pool.wait_ge(bias_loaded[c], 16 * (bt.n + 1))
                pool.tensor_tensor(region[bt.par][:, cols(c)], region[bt.par][:, cols(c)],
                                   f1_all[bt.par][:, cols(c)], ALU.add).then_inc(xb_done, 1)

            def step(bt):
                for t in range(NT):
                    scale_h(bt, t)
                    if t == NT - 2 and not is_first(bt):
                        add_bias(bt, 0)
                        add_bias(bt, 1)
                for c in range(0 if is_first(bt) else 2, NC):
                    add_bias(bt, c)

            pool.memset(ident[:, :], 0.0).then_inc(ident_set, 1)
            pool.wait_ge(ident_set, 1)
            pool.affine_select(out=ident[:, :], in_=ident[:, :], compare_op=ALU.not_equal, fill=1.0,
                               base=0, pattern=[[-1, P]], channel_multiplier=1).then_inc(ident_set, 1)
            steps(pool, step)


NEG_BIG = -3.4028234663852886e38


def kernel(x, adj, L0_gnn_W, L0_gnn_a1, L0_gnn_a2, L0_gnn_bias, L1_gnn_W, L1_gnn_b, L1_gnn_gamma, L1_gnn_beta):
    import numpy as np
    import concourse.bacc as bacc
    from concourse.bass_utils import run_bass_kernel_spmd

    def lay(a):
        return np.ascontiguousarray(a)

    x, adj, W = np.asarray(x), np.asarray(adj), np.asarray(L0_gnn_W)
    arrays = {
        "adjT": lay(adj.transpose(0, 2, 1)),
        "xT": lay(x.transpose(0, 2, 1)),
        "biasT": lay(np.asarray(L0_gnn_bias).T),
        "W": lay(W),
        "WT": lay(W.T),
        "a12": lay(np.concatenate([np.asarray(L0_gnn_a1), np.asarray(L0_gnn_a2)], axis=1)),
        "W1": lay(L1_gnn_W),
        "b1": lay(L1_gnn_b),
        "gamma": lay(np.asarray(L1_gnn_gamma).reshape(-1, 1)),
        "beta": lay(np.asarray(L1_gnn_beta).reshape(-1, 1)),
    }
    nc = bacc.Bacc("TRN2", target_bir_lowering=False, num_devices=1, dynamic_dma_scratch_size=SCRATCH)
    args = [nc.dram_tensor(name, a.shape, F32, kind="ExternalInput").ap() for name, a in arrays.items()]
    out = nc.dram_tensor("outT", arrays["xT"].shape, F32, kind="ExternalOutput").ap()
    build(nc, *args, out)
    r = run_bass_kernel_spmd(nc, [arrays], core_ids=[0])
    return np.ascontiguousarray(np.asarray(r.results[0]["outT"]).transpose(0, 2, 1))
```
